# Optimizing a Trainium2 kernel written in Bass

```python
import numpy as np
import jax
import jax.numpy as jnp

def _softmax(x, axis=-1):
    return jax.nn.softmax(x, axis=axis)
def _gelu(x):
    return jax.nn.gelu(x, approximate=True)
def _silu(x):
    return jax.nn.silu(x)
def _sigmoid(x):
    return jax.nn.sigmoid(x)
def _layernorm(x, axis=-1, eps=1e-5):
    m = jnp.mean(x, axis=axis, keepdims=True)
    v = jnp.var(x, axis=axis, keepdims=True)
    return (x - m) / jnp.sqrt(v + eps)
def _scatter_add(tgt, idx, src, axis=0):
    return tgt.at[idx].add(src)
def _segment_sum(src, seg, n):
    return jax.ops.segment_sum(src, seg, n)

kernel_name = 'mk_adj_preln_d4_adj_128_3a5abf'

def setup_inputs(seed: int = 0):
    np.random.seed(seed)
    _w = jnp.asarray
    def _rec_inputs():
        import jax
        import jax.numpy as jnp
        _gk = jax.random.key(seed)
        x = -0.0002928 + 1 * jax.random.normal(jax.random.fold_in(_gk, 1), (8, 2048, 128), jnp.float32)
        _a = jax.random.bernoulli(jax.random.fold_in(_gk, 2), 0.0078125, (8, 2048, 2048))
        _a = jnp.logical_or(_a, jnp.swapaxes(_a, -1, -2))
        _a = jnp.logical_or(_a, jnp.eye(2048, dtype=bool))
        _af = _a.astype(jnp.float32)
        _af = _af * jax.random.uniform(jax.random.fold_in(_gk, 3), (8, 2048, 2048), jnp.float32, 0.05, 1)
        adj = _af
        return x, adj
    x, adj = _rec_inputs()
    def _L0_gnn_setup():
        import jax, jax.numpy as jnp
        import numpy as np
        B, N, D, L = (16, 2048, 128, 3)
        LN_EPS = 1e-05

        def _layer_norm(z, gamma, beta):
            mu = jnp.mean(z, axis=-1, keepdims=True)
            var = jnp.mean(jnp.square(z - mu), axis=-1, keepdims=True)
            return (z - mu) * jax.lax.rsqrt(var + LN_EPS) * gamma + beta
        key = jax.random.key(seed)
        k_x, k_a, k_w = jax.random.split(key, 3)
        X = jax.random.normal(k_x, (B, N, D), dtype=jnp.float32)
        adj_mat = jax.random.uniform(k_a, (B, N, N), dtype=jnp.float32)
        limit = np.sqrt(6.0 / (D + D))
        Ws = jax.random.uniform(k_w, (L, D, D), dtype=jnp.float32, minval=-limit, maxval=limit)
        bs = jnp.zeros((L, D), dtype=jnp.float32)
        gammas = jnp.ones((L, D), dtype=jnp.float32)
        betas = jnp.zeros((L, D), dtype=jnp.float32)
        return {'X': X, 'adj_mat': adj_mat, 'Ws': Ws, 'bs': bs, 'gammas': gammas, 'betas': betas}
    _L0_gnn_all = _L0_gnn_setup()
    _L0_gnn_in = {k: v for k, v in _L0_gnn_all.items() if k in ('Ws', 'bs', 'gammas', 'betas', )}
    del _L0_gnn_all

    def _L1_gnn_setup():
        import jax, jax.numpy as jnp
        import numpy as np
        B, T, C_IN, C_OUT = (2, 1024, 128, 64)
        NEG_INF = -1e+22
        key = jax.random.key(seed)
        k_feat, k_adj, k_w1, k_w2, k_a = jax.random.split(key, 5)
        feat = jax.random.normal(k_feat, (B, T, C_IN), dtype=jnp.float32)
        adj = jax.random.randint(k_adj, (B, T, T), 0, 2).astype(jnp.float32)
        s_in = 1.0 / np.sqrt(C_IN)
        s_out = 1.0 / np.sqrt(C_OUT)
        W1 = jax.random.uniform(k_w1, (C_OUT, C_IN), jnp.float32, -s_in, s_in)
        W2 = jax.random.uniform(k_w2, (C_OUT, C_IN), jnp.float32, -s_in, s_in)
        a = jax.random.uniform(k_a, (C_OUT,), jnp.float32, -s_out, s_out)
        return {'feat': feat, 'adj': adj, 'W1': W1, 'W2': W2, 'a': a}
    _L1_gnn_all = _L1_gnn_setup()
    _L1_gnn_in = {k: v for k, v in _L1_gnn_all.items() if k in ('W1', 'W2', 'a', )}
    del _L1_gnn_all

    def _L2_gnn_setup():
        import jax, jax.numpy as jnp
        import numpy as np
        IN_DIM = 128
        OUT_DIM = 128
        NUM_HEADS = 4
        HEAD_DIM = OUT_DIM // NUM_HEADS
        B, N = (8, 2048)
        key = jax.random.key(seed)
        ks = jax.random.split(key, 12)
        s_in = 1.0 / np.sqrt(IN_DIM)
        s_out = 1.0 / np.sqrt(OUT_DIM)
        x = jax.random.normal(ks[0], (B, N, IN_DIM), dtype=jnp.float32)
        adj = jax.random.randint(ks[1], (B, N, N), 0, 2).astype(jnp.float32)
        return {'x': x, 'adj': adj, 'Wq': jax.random.uniform(ks[2], (IN_DIM, OUT_DIM), jnp.float32, -s_in, s_in), 'bq': jax.random.uniform(ks[3], (OUT_DIM,), jnp.float32, -s_in, s_in), 'Wk': jax.random.uniform(ks[4], (IN_DIM, OUT_DIM), jnp.float32, -s_in, s_in), 'bk': jax.random.uniform(ks[5], (OUT_DIM,), jnp.float32, -s_in, s_in), 'Wv': jax.random.uniform(ks[6], (IN_DIM, OUT_DIM), jnp.float32, -s_in, s_in), 'bv': jax.random.uniform(ks[7], (OUT_DIM,), jnp.float32, -s_in, s_in), 'Wo': jax.random.uniform(ks[8], (OUT_DIM, OUT_DIM), jnp.float32, -s_out, s_out), 'bo': jax.random.uniform(ks[9], (OUT_DIM,), jnp.float32, -s_out, s_out)}
    _L2_gnn_all = _L2_gnn_setup()
    _L2_gnn_in = {k: v for k, v in _L2_gnn_all.items() if k in ('Wq', 'bq', 'Wk', 'bk', 'Wv', 'bv', 'Wo', 'bo', )}
    del _L2_gnn_all

    def _L3_gnn_setup():
        import jax, jax.numpy as jnp
        import numpy as np
        key = jax.random.key(seed)
        k1, k2, k3 = jax.random.split(key, 3)
        B_, N, F, O = (8, 2048, 128, 128)
        H = jax.random.normal(k1, (B_, N, F), dtype=jnp.float32)
        A = jax.random.uniform(k2, (B_, N, N), dtype=jnp.float32)
        B = jax.random.normal(k3, (F, O), dtype=jnp.float32) / np.sqrt(F)
        return {'H': H, 'A': A, 'B': B}
    _L3_gnn_all = _L3_gnn_setup()
    _L3_gnn_in = {k: v for k, v in _L3_gnn_all.items() if k in ('B', )}
    del _L3_gnn_all

    return {
        "x": x,
        "adj": adj,
        "L0_gnn_Ws": _L0_gnn_in["Ws"],
        "L0_gnn_bs": _L0_gnn_in["bs"],
        "L0_gnn_gammas": _L0_gnn_in["gammas"],
        "L0_gnn_betas": _L0_gnn_in["betas"],
        "L1_gnn_W1": _L1_gnn_in["W1"],
        "L1_gnn_W2": _L1_gnn_in["W2"],
        "L1_gnn_a": _L1_gnn_in["a"],
        "L2_gnn_Wq": _L2_gnn_in["Wq"],
        "L2_gnn_bq": _L2_gnn_in["bq"],
        "L2_gnn_Wk": _L2_gnn_in["Wk"],
        "L2_gnn_bk": _L2_gnn_in["bk"],
        "L2_gnn_Wv": _L2_gnn_in["Wv"],
        "L2_gnn_bv": _L2_gnn_in["bv"],
        "L2_gnn_Wo": _L2_gnn_in["Wo"],
        "L2_gnn_bo": _L2_gnn_in["bo"],
        "L3_gnn_B": _L3_gnn_in["B"],
    }

def reference(x, adj, L0_gnn_Ws, L0_gnn_bs, L0_gnn_gammas, L0_gnn_betas, L1_gnn_W1, L1_gnn_W2, L1_gnn_a, L2_gnn_Wq, L2_gnn_bq, L2_gnn_Wk, L2_gnn_bk, L2_gnn_Wv, L2_gnn_bv, L2_gnn_Wo, L2_gnn_bo, L3_gnn_B):
    import jax
    import jax.numpy as jnp
    def _L0_gnn_ref(X, adj_mat, Ws, bs, gammas, betas):
        import jax, jax.numpy as jnp
        import numpy as np
        B, N, D, L = (16, 2048, 128, 3)
        LN_EPS = 1e-05

        def _layer_norm(z, gamma, beta):
            mu = jnp.mean(z, axis=-1, keepdims=True)
            var = jnp.mean(jnp.square(z - mu), axis=-1, keepdims=True)
            return (z - mu) * jax.lax.rsqrt(var + LN_EPS) * gamma + beta
        h = X
        for i in range(L):
            res = h
            hw = jnp.einsum('bnd,de->bne', h, Ws[i])
            agg = jnp.einsum('bij,bie->bje', adj_mat, hw)
            conv = agg + bs[i]
            h = jax.nn.relu(_layer_norm(conv + res, gammas[i], betas[i]))
        return h

    def _L1_gnn_ref(feat, adj, W1, W2, a):
        import jax, jax.numpy as jnp
        import numpy as np
        B, T, C_IN, C_OUT = (2, 1024, 128, 64)
        NEG_INF = -1e+22
        mask = jnp.where(adj > 0, jnp.float32(0.0), jnp.float32(NEG_INF))
        q = feat @ W1.T
        k = feat @ W2.T
        e = jax.nn.relu(q[:, None, :, :] + k[:, :, None, :])
        scores = jnp.einsum('bijd,d->bij', e, a)
        att = jax.nn.softmax(scores + mask, axis=-1)
        return att @ feat

    def _L2_gnn_ref(x, adj, Wq, bq, Wk, bk, Wv, bv, Wo, bo):
        import jax, jax.numpy as jnp
        import numpy as np
        IN_DIM = 128
        OUT_DIM = 128
        NUM_HEADS = 4
        HEAD_DIM = OUT_DIM // NUM_HEADS
        B, N = (8, 2048)
        Bs, Ns, _ = x.shape
        scale = jnp.sqrt(jnp.asarray(HEAD_DIM, dtype=x.dtype))
        Q = (x @ Wq + bq).reshape(Bs, Ns, NUM_HEADS, HEAD_DIM)
        K = (x @ Wk + bk).reshape(Bs, Ns, NUM_HEADS, HEAD_DIM)
        V = (x @ Wv + bv).reshape(Bs, Ns, NUM_HEADS, HEAD_DIM)
        scores = jnp.einsum('bnhd,bmhd->bhnm', Q, K) / scale
        scores = scores + (1.0 - adj[:, None, :, :]) * -1000000000.0
        attn = jax.nn.softmax(scores, axis=-1)
        out = jnp.einsum('bhnm,bmhd->bnhd', attn, V).reshape(Bs, Ns, OUT_DIM)
        return out @ Wo + bo

    def _L3_gnn_ref(H, A, B):
        import jax, jax.numpy as jnp
        import numpy as np
        N = A.shape[-1]
        A1 = A + jnp.eye(N, dtype=A.dtype)
        deg = jnp.sum(A1, axis=-1)
        d = jax.lax.rsqrt(deg)
        A_norm = A1 * d[:, :, None] * d[:, None, :]
        HB = jnp.matmul(A_norm, H)
        return jnp.matmul(HB, B)

    h = jnp.maximum(_layernorm(x, axis=-1), 0.0)
    x = x + _L0_gnn_ref(h, adj, L0_gnn_Ws, L0_gnn_bs, L0_gnn_gammas, L0_gnn_betas)
    h = jnp.maximum(_layernorm(x, axis=-1), 0.0)
    x = x + _L1_gnn_ref(h, adj, L1_gnn_W1, L1_gnn_W2, L1_gnn_a)
    h = jnp.maximum(_layernorm(x, axis=-1), 0.0)
    x = x + _L2_gnn_ref(h, adj, L2_gnn_Wq, L2_gnn_bq, L2_gnn_Wk, L2_gnn_bk, L2_gnn_Wv, L2_gnn_bv, L2_gnn_Wo, L2_gnn_bo)
    h = jnp.maximum(_layernorm(x, axis=-1), 0.0)
    x = x + _L3_gnn_ref(h, adj, L3_gnn_B)
    return x


_drawn_inputs = setup_inputs


def setup_inputs(seed=0):
    import zlib

    import numpy as np

    out = dict(_drawn_inputs(seed))
    spreads = {'L0_gnn_bs': (0.0, 0.692), 'L0_gnn_gammas': (1.0, 0.2), 'L0_gnn_betas': (0.0, 0.1)}
    factors = {'L1_gnn_W1': 8.0, 'L1_gnn_W2': 8.0, 'L1_gnn_a': 8.0, 'L2_gnn_bv': 3.173}
    for name, (base, spread) in spreads.items():
        noise = np.random.default_rng([zlib.crc32(name.encode()), seed]).standard_normal(out[name].shape)
        drawn = base * np.exp(spread * noise) if base else spread * noise
        out[name] = jnp.asarray(drawn.astype(out[name].dtype))
    for name, factor in factors.items():
        out[name] = (out[name] * factor).astype(out[name].dtype)
    return out
```

```python
from contextlib import ExitStack

import concourse.bass as bass
from concourse import mybir

F32 = mybir.dt.float32
F32R = mybir.dt.float32r
ALU = mybir.AluOpType
ACT = mybir.ActivationFunctionType

P = 128
NB, N, D = 8, 2048, 128
NT = N // P
CH = 512
NC = N // CH
TPC = NT // NC
LAYERS = 3
HEADS, HD = 4, 32
DG = 64
QUADS = 16
QROWS = P // 4
LN_EPS = 1e-5
BIG = 3.0e38
MASK_ADD = 1e22
MASK_DOT = 1e9
SCALE = float(1.0 / (HD ** 0.5))
LNS = LAYERS + 4
HTS = LAYERS + 2


class Steps:

    def __init__(self, sem, per_batch):
        self.sem, self.per_batch, self.k = sem, per_batch, 0

    def done(self, ins):
        self.k += 1
        ins.then_inc(self.sem, 1)

    def wait(self, eng, b):
        eng.wait_ge(self.sem, b * self.per_batch + self.k)


def build(nc, x, adj, Ws, bs, gammas, betas, W1, W2, a_vec, Wq, bq, Wk, bk, Wv, bv, Wo, bo, Bw, out):
    x_v = x.rearrange("b (t p) d -> b p t d", p=P)
    out_v = out.rearrange("b (t p) d -> b p t d", p=P)
    adj_v = adj.rearrange("b (t p) n -> b t p n", p=P)

    with ExitStack() as ctx:
        def sb(name, shape, dt=F32, where=None):
            return (where or ctx).enter_context(nc.sbuf_tensor(name, shape, dt))

        def sem(name):
            return ctx.enter_context(nc.semaphore(name))

        ring = sb("adj_ring", [P, 2, N])
        X = sb("X", [P, NT, D])
        H = sb("H", [P, NT, D])
        HT = sb("HT", [P, N])
        HW = sb("HW", [P, N])
        AGG = sb("AGG", [P, N])
        ident = sb("ident", [P, P])
        w0 = sb("w0", [P, LAYERS, D])
        b0 = sb("b0", [P, LAYERS])
        gam = sb("gam", [P, LAYERS, D])
        bet = sb("bet", [P, LAYERS, D])
        w12 = sb("w12", [P, D])
        w1t2 = sb("w1t2", [P, P])
        w2t = sb("w2t", [P, DG])
        a_col = sb("a_col", [P, 1])
        a_win = sb("a_win", [P, 2 * QROWS - 2])
        wq = sb("wq", [P, D])
        wk = sb("wk", [P, D])
        wv = sb("wv", [P, D])
        wo = sb("wo", [P, D])
        wb = sb("wb", [P, D])
        bq_c = sb("bq_c", [P, 1])
        bqs_c = sb("bqs_c", [P, 1])
        bk_c = sb("bk_c", [P, 1])
        bv_b = sb("bv_b", [P, D])
        bo_b = sb("bo_b", [P, D])
        halves = sb("halves", [P, NT])
        epses = sb("epses", [P, NT])
        ones = sb("ones", [P, NT])
        stats = sb("stats", [P, NT, 6])
        mv = sb("mv", [P, NT, 2])
        var = sb("var", [P, NT])
        rstd = sb("rstd", [P, NT])
        deg = sb("deg", [P, NT])
        deg1 = sb("deg1", [P, NT])
        dinv = sb("dinv", [P, NT])
        kd = sb("kd", [P, 2, 64])
        ka = sb("ka", [P, 2, 64])
        nmin1 = sb("nmin1", [P, 2])
        rsum1 = sb("rsum1", [P, 2])
        rinv1 = sb("rinv1", [P, 2])
        nmin2 = sb("nmin2", [P, HEADS])
        rsum2 = sb("rsum2", [P, HEADS])
        rinv2 = sb("rinv2", [P, HEADS])
        qcur = sb("qcur", [P, HEADS, P], F32R)
        hbT = sb("hbT", [P, 2, P])

        with ExitStack() as ph:
            A = sb("adj_res", [P, NT, N], where=ph)
        with ExitStack() as ph:
            E = sb("E", [P, 8, N], where=ph)
            Q2 = sb("Q2", [P, N], where=ph)
            K2 = sb("K2", [P, N // 2], where=ph)
            T1 = sb("T1", [P, N], where=ph)
            PT1 = sb("PT1", [P, N], where=ph)
        with ExitStack() as ph:
            kst = sb("kst", [P, HEADS, N], F32R, where=ph)
            qst = sb("qst", [P, HEADS, N], F32R, where=ph)
            V = sb("V", [P, NT, D], where=ph)
            M2 = sb("M2", [P, N], where=ph)
            PT2 = sb("PT2", [P, NC, CH], where=ph)
            with ExitStack() as sub:
                T2 = sb("T2", [P, HEADS, N], where=sub)
            with ExitStack() as sub:
                qh = sb("qh", [P, N], F32R, where=sub)
                ql = sb("ql", [P, N], F32R, where=sub)
                kh = sb("kh", [P, N], F32R, where=sub)
                kl = sb("kl", [P, N], F32R, where=sub)

        ps = ctx.enter_context(nc.psum_tensor("ps", [P, 8, CH], F32))

        waited = sem("waited")
        const_in = sem("const_in")
        const_w = sem("const_w")
        w12_ps = sem("w12_ps")
        const_rdy = sem("const_rdy")
        id_rdy = sem("id_rdy")
        x_in = sem("x_in")
        adj_in = sem("adj_in")
        ring_in = [sem("ring_in0"), sem("ring_in1")]
        ring_free = sem("ring_free")
        dve_self = sem("dve_self")
        pool_self = sem("pool_self")
        ln_stats = sem("ln_stats")
        ln_rstd = sem("ln_rstd")
        deg_rdy = sem("deg_rdy")
        dinv_rdy = sem("dinv_rdy")
        h_rdy = sem("h_rdy")
        ht_ps = sem("ht_ps")
        ht_sb = sem("ht_sb")
        hw_ps = sem("hw_ps")
        hw_sb = sem("hw_sb")
        agg_ps = sem("agg_ps")
        agg_sb = sem("agg_sb")
        z_ps = sem("z_ps")
        qk1_ps = sem("qk1_ps")
        qk1_sb = sem("qk1_sb")
        kd_rdy = sem("kd_rdy")
        ka_rdy = sem("ka_rdy")
        e_dve = sem("e_dve")
        e_act = sem("e_act")
        e_used = sem("e_used")
        mask1 = sem("mask1")
        t1_rdy = sem("t1_rdy")
        p1_rdy = sem("p1_rdy")
        pt1_ps = sem("pt1_ps")
        pt1_act = sem("pt1_act")
        pt1_dve = sem("pt1_dve")
        rinv1_rdy = sem("rinv1_rdy")
        o1_ps = sem("o1_ps")
        x2_rdy = sem("x2_rdy")
        qk2_ps = sem("qk2_ps")
        qk2_act = sem("qk2_act")
        qk2_dve = sem("qk2_dve")
        v_ps = sem("v_ps")
        v_sb = sem("v_sb")
        st_in = sem("st_in")
        qcur_rdy = sem("qcur_rdy")
        s2_ps = sem("s2_ps")
        t2_rdy = sem("t2_rdy")
        p2_rdy = sem("p2_rdy")
        pt2_ps = sem("pt2_ps")
        pt2_act = sem("pt2_act")
        pt2_dve = sem("pt2_dve")
        rinv2_rdy = sem("rinv2_rdy")
        o2_ps = sem("o2_ps")
        att_rdy = sem("att_rdy")
        at_ps = sem("at_ps")
        at_sb = sem("at_sb")
        x3_ps = sem("x3_ps")
        diag_rdy = sem("diag_rdy")
        at3_ps = sem("at3_ps")
        at3_act = sem("at3_act")
        at3_dve = sem("at3_dve")
        hb_ps = sem("hb_ps")
        hb_sb = sem("hb_sb")
        o3_ps = sem("o3_ps")
        o3_rdy = sem("o3_rdy")
        out_done = sem("out_done")

        CONST_DMAS = 16
        block = ctx.enter_context(nc.Block())

        def alone(eng):
            eng.sem_inc(waited, 1)

        def tcols(t):
            return bass.ds(t * P, P)

        @block.sync
        def _(sp):
            def const(dst, src):
                sp.dma_start(dst, src).then_inc(const_in, 16)

            def bcast(src, n):
                return src.rearrange("(o e) -> o e", o=1).broadcast_to([P, n])

            const(w0[:, :, :], Ws.rearrange("l d e -> d l e"))
            with nc.allow_non_contiguous_dma(reason="one small load"):
                const(b0[:, :], bs.rearrange("l e -> e l"))
            const(gam[:, :, :].rearrange("p l e -> p (l e)"), bcast(gammas.rearrange("l e -> (l e)"), LAYERS * D))
            const(bet[:, :, :].rearrange("p l e -> p (l e)"), bcast(betas.rearrange("l e -> (l e)"), LAYERS * D))
            const(w12[0:DG, :], W1)
            const(w12[DG:P, :], W2)
            const(a_col[0:DG, :], a_vec.rearrange("(e o) -> e o", o=1))
            const(a_col[DG:P, :], a_vec.rearrange("(e o) -> e o", o=1))
            for dst, src in ((wq, Wq), (wk, Wk), (wv, Wv), (wo, Wo), (wb, Bw)):
                const(dst[:, :], src)
            const(bq_c[:, :], bq.rearrange("(e o) -> e o", o=1))
            const(bk_c[:, :], bk.rearrange("(e o) -> e o", o=1))
            const(bo_b[:, :], bcast(bo, D))
            sp.dma_start(bv_b[:, :], bcast(bv, D)).then_inc(out_done, 16)
            with sp.Fori(0, NB) as b:
                sp.wait_ge(o3_rdy, b * NT + 3)
                for t in range(NT):
                    sp.dma_start(X[:, t, :], x_v[bass.ds(b, 1), :, t].rearrange("o p d -> p (o d)")).then_inc(x_in, 16)
                for phase in range(3):
                    with sp.Fori(0, NT // 2) as tt:
                        for u in range(2):
                            sp.wait_ge(ring_free, b * (3 * NT) + tt * 2 + (phase * NT + u + 1))
                            sp.dma_start(ring[:, u, :],
                                         adj_v[bass.ds(b, 1), bass.ds(tt * 2 + u, 1)].rearrange("o c p n -> p (o c n)")
                                         ).then_inc(ring_in[u], 16)
                sp.wait_ge(o3_rdy, b * NT + (NT + 3))
                sp.dma_start(out_v[bass.ds(b, 1)].rearrange("o p t d -> p (o t) d"),
                             HW[:, :].rearrange("p (t d) -> p t d", t=NT)).then_inc(out_done, 16)
            sp.wait_ge(out_done, 16 * (NB + 1))

        def ring_wait(eng, b, phase, half, u):
            eng.wait_ge(ring_in[u], b * (16 * 24) + half * 16 + 16 * (phase * 8 + 1))

        @block.gpsimd
        def _(pool):
            pool.memset(ident[:, :], 0.0).then_inc(pool_self, 1)
            pool.memset(halves[:, :], -0.5).then_inc(pool_self, 1)
            pool.memset(epses[:, :], LN_EPS).then_inc(pool_self, 1)
            pool.memset(ones[:, :], 1.0).then_inc(pool_self, 1)
            pool.wait_ge(pool_self, 4)
            pool.affine_select(out=ident[:, :], in_=ident[:, :], compare_op=ALU.not_equal, fill=1.0, base=0,
                               pattern=[[-1, P]], channel_multiplier=1).then_inc(id_rdy, 1)
            own = Steps(pool_self, LNS + 1)
            own.k = 4

            def rstd_step(b, i):
                pool.wait_ge(ln_stats, b * LNS + i + 1)
                own.done(pool.tensor_tensor(var[:, :], mv[:, :, 1], epses[:, :], ALU.add))
                own.wait(pool, b)
                pool.tensor_tensor(rstd[:, :], var[:, :], halves[:, :], ALU.pow).then_inc(ln_rstd, 1)

            with pool.Fori(0, NB) as b:
                own.k = 4
                for t in range(NT):
                    pool.dma_start(A[:, t, :], adj_v[bass.ds(b, 1), t].rearrange("o p n -> p (o n)")).then_inc(adj_in, 16)
                rstd_step(b, 0)
                pool.wait_ge(deg_rdy, (b + 1) * NT)
                own.done(pool.tensor_tensor(deg1[:, :], deg[:, :], ones[:, :], ALU.add))
                own.wait(pool, b)
                pool.tensor_tensor(dinv[:, :], deg1[:, :], halves[:, :], ALU.pow).then_inc(dinv_rdy, 1)
                for i in range(1, LNS):
                    rstd_step(b, i)

        @block.scalar
        def _(act):
            def evac(dst, src):
                return nc.scalar.activation(dst, src, ACT.Copy)

            def evac_ht(b, i):
                for c in range(NC):
                    act.wait_ge(ht_ps, b * (HTS * NC) + i * NC + c + 1)
                    evac(HT[:, c * CH:(c + 1) * CH], ps[:, c, :]).then_inc(ht_sb, 1)

            def keys(t, T, u, first):
                if not first:
                    act.wait_ge(e_act, (T - 1) * QUADS)
                evac(ka[:, u, :], K2[:, bass.ds(t * 64, 64)]).then_inc(ka_rdy, 1)
                act.wait_ge(ka_rdy, T + 1)

            def quad(T, m, u, first):
                if not (first and m < 2):
                    act.wait_ge(e_used, T * QUADS + (m - 1))
                s = 4 * (m % 2)
                nc.scalar.activation(E[:, s + 2, N // 2:N], Q2[:, N // 2:N], ACT.Relu, bias=ka[:, u, 32 + m:33 + m])
                nc.scalar.activation(E[:, s + 3, :], Q2[:, :], ACT.Relu, bias=ka[:, u, 48 + m:49 + m]).then_inc(e_act, 1)

            def exp1(T, u):
                act.wait_ge(t1_rdy, T + 1)
                nc.scalar.activation(T1[:, :], T1[:, :], ACT.Exp, bias=nmin1[:, u:u + 1], scale=-1.0,
                                     accum_out=rsum1[:, u:u + 1]).then_inc(p1_rdy, 1)

            def evac1(T, u):
                for g in range(2):
                    act.wait_ge(pt1_ps, T * NC + g + 1)
                    last = evac(PT1[:, g * CH:(g + 1) * CH], ps[:, 4 * u + g, :])
                last.then_inc(pt1_act, 1)

            def tile1(b, t, u, tail, first):
                T = b * NT + t
                keys(t, T, u, first)
                for m in range(QUADS):
                    quad(T, m, u, not tail)
                    if tail and m == 3:
                        exp1(T - 1, 1 - u)
                    if tail and m == 6:
                        evac1(T - 1, 1 - u)

            def exp2(s, h):
                act.wait_ge(t2_rdy, s + 1)
                nc.scalar.activation(T2[:, h, :], T2[:, h, :], ACT.Exp, bias=nmin2[:, h:h + 1], scale=-1.0,
                                     accum_out=rsum2[:, h:h + 1]).then_inc(p2_rdy, 1)

            def evac2(r):
                for g in range(2):
                    act.wait_ge(pt2_ps, r * NC + g + 1)
                    evac(PT2[:, g, :], ps[:, 4 + g, :]).then_inc(pt2_act, 1)

            act.wait_ge(const_rdy, 1)
            with act.Fori(0, NB) as b:
                act.wait_ge(out_done, b * 16 + 16)
                for l in range(LAYERS):
                    evac_ht(b, l)
                    for g in range(NC):
                        act.wait_ge(hw_ps, b * (LAYERS * NC) + l * NC + g + 1)
                        evac(HW[:, g * CH:(g + 1) * CH], ps[:, 4 + g, :]).then_inc(hw_sb, 1)
                    if l == 0:
                        act.wait_ge(adj_in, (b + 1) * (16 * NT))
                        act.wait_ge(hw_sb, b * (LAYERS * NC) + NC)
                        for t in range(NT):
                            nc.scalar.activation(ps[:, 4:8, :].rearrange("p c n -> p (c n)"), A[:, t, :], ACT.Copy,
                                                 accum_out=deg[:, t:t + 1]).then_inc(deg_rdy, 1)
                            act.wait_ge(deg_rdy, b * NT + t + 1)
                    for c in range(NC):
                        act.wait_ge(agg_ps, b * (LAYERS * NC) + l * NC + c + 1)
                        nc.scalar.activation(AGG[:, c * CH:(c + 1) * CH], ps[:, c, :], ACT.Identity,
                                             bias=b0[:, l:l + 1]).then_inc(agg_sb, 1)
                evac_ht(b, LAYERS)
                for c in range(NC):
                    act.wait_ge(qk1_ps, b * 6 + c + 1)
                    evac(Q2[:, c * CH:(c + 1) * CH], ps[:, 4 + c, :]).then_inc(qk1_sb, 1)
                for c in range(2):
                    act.wait_ge(qk1_ps, b * 6 + 4 + c + 1)
                    evac(K2[:, c * CH:(c + 1) * CH], ps[:, c, :]).then_inc(qk1_sb, 1)
                act.wait_ge(qk1_sb, (b + 1) * 6)
                tile1(b, 0, 0, False, True)
                tile1(b, 1, 1, True, True)
                with act.Fori(1, NT // 2) as tt:
                    tile1(b, tt * 2, 0, True, False)
                    tile1(b, tt * 2 + 1, 1, True, False)
                exp1(b * NT + NT - 1, 1)
                evac1(b * NT + NT - 1, 1)
                evac_ht(b, LAYERS + 1)
                for c in range(NC):
                    act.wait_ge(qk2_ps, b * 8 + c + 1)
                    nc.scalar.activation(HW[:, c * CH:(c + 1) * CH], ps[:, 4 + c, :], ACT.Identity,
                                         bias=bqs_c[:, 0:1], scale=-SCALE).then_inc(qk2_act, 1)
                for c in range(NC):
                    act.wait_ge(qk2_ps, b * 8 + 4 + c + 1)
                    nc.scalar.activation(AGG[:, c * CH:(c + 1) * CH], ps[:, c, :], ACT.Identity,
                                         bias=bk_c[:, 0:1]).then_inc(qk2_act, 1)
                for dst, parts, k in ((qst, (qh, qh, ql, ql), 1), (kst, (kh, kl, kh, kl), 2)):
                    act.wait_ge(qk2_dve, b * 2 + k)
                    for h in range(HEADS):
                        for blk in range(4):
                            act.dma_start(dst[HD * blk:HD * (blk + 1), h, :].bitcast(F32),
                                          parts[blk][HD * h:HD * (h + 1), :].bitcast(F32)).then_inc(st_in, 16)
                S0 = b * (NT * HEADS)
                exp2(S0, 0)
                exp2(S0 + 1, 1)
                for h in range(2, HEADS):
                    exp2(S0 + h, h)
                    evac2(S0 + h - 2)
                with act.Fori(1, NT) as t:
                    for h in range(HEADS):
                        s = S0 + t * HEADS + h
                        exp2(s, h)
                        evac2(s - 2)
                for r in (NT * HEADS - 2, NT * HEADS - 1):
                    evac2(S0 + r)
                for c in range(NC):
                    act.wait_ge(at_ps, b * NC + c + 1)
                    evac(HT[:, c * CH:(c + 1) * CH], ps[:, c, :]).then_inc(at_sb, 1)
                with act.Fori(0, NT // 2) as tt:
                    for u in range(2):
                        T = b * NT + tt * 2 + u
                        AT = (AGG, HT)[u]
                        for g in range(2):
                            act.wait_ge(at3_ps, T * NC + g + 1)
                            evac(AT[:, g * CH:(g + 1) * CH], ps[:, (4 * u + g) % 6, :]).then_inc(at3_act, 1)
                    for u in range(2):
                        T = b * NT + tt * 2 + u
                        act.wait_ge(hb_ps, T + 1)
                        evac(hbT[:, u, :], ps[:, 6 + u, 0:P]).then_inc(hb_sb, 1)

        @block.vector
        def _(dve):
            own = Steps(dve_self, 4 * LNS + 1)

            def link(b, ins):
                own.done(ins)
                own.wait(dve, b)

            nc.vector.memset(a_win[:, :], 0.0).then_inc(ring_free, 1)
            nc.vector.memset(mv[:, :, :], 0.0).then_inc(ring_free, 1)
            for buf in (stats[:, :, :], dinv[:, :], rstd[:, :]):
                nc.vector.memset(buf, 0.0).then_inc(o3_rdy, 1)
            dve.wait_ge(ring_free, 2)
            dve.wait_ge(o3_rdy, 3)
            dve.wait_ge(out_done, 16)
            dve.wait_ge(const_in, 16 * CONST_DMAS)
            nc.vector.tensor_scalar(a_win[0:DG, QROWS - 2:QROWS - 1], a_col[0:DG, :], -1.0, None, ALU.mult)
            nc.vector.tensor_scalar(a_win[DG:P, QROWS - 1:QROWS], a_col[DG:P, :], -1.0, None, ALU.mult)
            nc.vector.tensor_scalar(bqs_c[:, :], bq_c[:, :], -SCALE, None, ALU.mult)
            dve.wait_ge(w12_ps, 1)
            nc.vector.tensor_copy(w1t2[:, 0:DG], ps[:, 0, 0:DG])
            nc.vector.tensor_copy(w1t2[:, DG:P], ps[:, 0, 0:DG])
            nc.vector.tensor_copy(w2t[:, :], ps[:, 0, DG:P]).then_inc(const_rdy, 1)

            def layer_norm(b, i, src, dst):
                for t in range(NT):
                    last = nc.vector.bn_stats(stats[:, t, :], src[:, t, :])
                link(b, last)
                alone(dve)
                for t in range(NT):
                    last = nc.vector.bn_aggr(mv[:, t, :], stats[:, t, :])
                last.then_inc(ln_stats, 1)
                dve.wait_ge(ln_rstd, b * LNS + i + 1)
                for t in range(NT):
                    last = nc.vector.tensor_scalar(dst[:, t, :], src[:, t, :], mv[:, t, 0:1], rstd[:, t:t + 1],
                                                   ALU.subtract, ALU.mult)
                link(b, last)

            def relu(dst):
                return nc.vector.tensor_scalar(dst, dst, 0.0, None, ALU.max)

            def tiles(buf):
                return buf[:, :].rearrange("p (t d) -> p t d", t=NT)

            def over_tiles(row):
                return row.rearrange("p (o d) -> p o d", o=1).broadcast_to([P, NT, D])

            def keys(t, T, u, first):
                if not first:
                    dve.wait_ge(e_dve, (T - 1) * QUADS)
                nc.vector.tensor_copy(kd[:, u, :], K2[:, bass.ds(t * 64, 64)]).then_inc(kd_rdy, 1)
                dve.wait_ge(kd_rdy, T + 1)

            def quad(T, m, u, first):
                if not (first and m < 2):
                    dve.wait_ge(e_used, T * QUADS + (m - 1))
                s = 4 * (m % 2)
                nc.vector.tensor_scalar(E[:, s, :], Q2[:, :], kd[:, u, m:m + 1], 0.0, ALU.add, ALU.max)
                nc.vector.tensor_scalar(E[:, s + 1, :], Q2[:, :], kd[:, u, 16 + m:17 + m], 0.0, ALU.add, ALU.max)
                nc.vector.tensor_scalar(E[:, s + 2, 0:N // 2], Q2[:, 0:N // 2], kd[:, u, 32 + m:33 + m], 0.0,
                                        ALU.add, ALU.max).then_inc(e_dve, 1)

            def mask_min1(b, T, half, u):
                dve.wait_ge(e_used, (T + 1) * QUADS)
                ring_wait(dve, b, 0, half, u)
                nc.vector.tensor_scalar(ring[:, u, :], ring[:, u, :], 0.0, MASK_ADD, ALU.is_le, ALU.mult
                                        ).then_inc(mask1, 1)
                dve.wait_ge(mask1, T + 1)
                alone(dve)
                nc.vector.tensor_tensor_reduce(
                    out=T1[:, :], in0=ps[:, 4 * u:4 * u + 4, :].rearrange("p c n -> p (c n)"), in1=ring[:, u, :],
                    scale=1.0, scalar=BIG, op0=ALU.add, op1=ALU.min, accum_out=nmin1[:, u:u + 1]
                ).then_inc(t1_rdy, 1)
                dve.wait_ge(t1_rdy, T + 1)
                dve.sem_inc(ring_free, 1)

            def evac1(T, u):
                for g in range(2, 4):
                    dve.wait_ge(pt1_ps, T * NC + g + 1)
                    last = nc.vector.tensor_copy(PT1[:, g * CH:(g + 1) * CH], ps[:, 4 * u + g, :])
                last.then_inc(pt1_dve, 1)

            def finish1(t, T, u):
                dve.wait_ge(p1_rdy, T + 1)
                nc.vector.reciprocal(rinv1[:, u:u + 1], rsum1[:, u:u + 1]).then_inc(rinv1_rdy, 1)
                dve.wait_ge(rinv1_rdy, T + 1)
                dve.wait_ge(o1_ps, T + 1)
                xt = X[:, bass.ds(t, 1), :].rearrange("p o d -> p (o d)")
                nc.vector.scalar_tensor_tensor(out=xt, in0=ps[:, 4 * u, 0:D], scalar=rinv1[:, u:u + 1], in1=xt,
                                               op0=ALU.mult, op1=ALU.add).then_inc(x2_rdy, 1)

            def tile1(b, t, u, tail, half, first):
                T = b * NT + t
                keys(t, T, u, first)
                for m in range(QUADS):
                    quad(T, m, u, not tail)
                    if tail and m == 1:
                        mask_min1(b, T - 1, half, 1 - u)
                    if tail and m == 6:
                        evac1(T - 1, 1 - u)
                    if tail and m == 11:
                        finish1(t - 1, T - 1, 1 - u)

            def mask_tile2(b, t, half, u):
                T = b * NT + t
                nc.vector.tensor_copy(qcur[:, :, :], qst[:, :, tcols(t)].bitcast(F32)).then_inc(qcur_rdy, 1)
                ring_wait(dve, b, 1, half, u)
                nc.vector.tensor_scalar(M2[:, :], ring[:, u, :], 1.0, -MASK_DOT, ALU.subtract, ALU.mult
                                        ).then_inc(ring_free, 1)
                dve.wait_ge(ring_free, b * (3 * NT) + t + (NT + 2 + 1))

            def min2(s, h):
                dve.wait_ge(s2_ps, s + 1)
                alone(dve)
                nc.vector.tensor_tensor_reduce(
                    out=T2[:, h, :], in0=ps[:, 0:4, :].rearrange("p c n -> p (c n)"), in1=M2[:, :],
                    scale=1.0, scalar=BIG, op0=ALU.add, op1=ALU.min, accum_out=nmin2[:, h:h + 1]
                ).then_inc(t2_rdy, 1)

            def evac2(r):
                for g in range(2, 4):
                    dve.wait_ge(pt2_ps, r * NC + g + 1)
                    nc.vector.tensor_copy(PT2[:, g, :], ps[:, 4 + g % 2, :]).then_inc(pt2_dve, 1)

            def finish2(t, r, h):
                dve.wait_ge(p2_rdy, r + 1)
                nc.vector.reciprocal(rinv2[:, h:h + 1], rsum2[:, h:h + 1]).then_inc(rinv2_rdy, 1)
                dve.wait_ge(rinv2_rdy, r + 1)
                dve.wait_ge(o2_ps, r + 1)
                dst = H[:, bass.ds(t, 1), h * HD:(h + 1) * HD].rearrange("p o d -> p (o d)")
                nc.vector.tensor_scalar(dst, ps[:, 6 + h % 2, 0:HD], rinv2[:, h:h + 1], None, ALU.mult
                                        ).then_inc(att_rdy, 1)

            own.k = 0
            with dve.Fori(0, NB) as b:
                dve.wait_ge(x_in, (b + 1) * (16 * NT))
                layer_norm(b, 0, X, H)
                relu(H[:, :, :]).then_inc(h_rdy, 1)
                for l in range(LAYERS):
                    Z = tiles(HT)
                    for g in range(NC):
                        dve.wait_ge(z_ps, b * (LAYERS * NC) + l * NC + g + 1)
                        last = nc.vector.tensor_tensor(
                            Z[:, g * TPC:(g + 1) * TPC, :],
                            ps[:, 4 + g, :].rearrange("p (t d) -> p t d", d=D),
                            H[:, g * TPC:(g + 1) * TPC, :], ALU.add)
                    link(b, last)
                    layer_norm(b, l + 1, Z, Z)
                    link(b, nc.vector.tensor_tensor(Z, Z, over_tiles(gam[:, l, :]), ALU.mult))
                    link(b, nc.vector.tensor_tensor(Z, Z, over_tiles(bet[:, l, :]), ALU.add))
                    last = nc.vector.tensor_scalar(H[:, :, :], Z, 0.0, None, ALU.max)
                    if l < LAYERS - 1:
                        last.then_inc(h_rdy, 1)
                        dve.wait_ge(h_rdy, b * HTS + l + 2)
                link(b, last)
                link(b, nc.vector.tensor_tensor(X[:, :, :], X[:, :, :], H[:, :, :], ALU.add))
                layer_norm(b, LAYERS + 1, X, H)
                relu(H[:, :, :]).then_inc(h_rdy, 1)
                dve.wait_ge(qk1_sb, (b + 1) * 6)
                tile1(b, 0, 0, False, 0, True)
                tile1(b, 1, 1, True, 0, True)
                with dve.Fori(1, NT // 2) as tt:
                    tile1(b, tt * 2, 0, True, tt - 1, False)
                    tile1(b, tt * 2 + 1, 1, True, tt, False)
                T = b * NT + NT - 1
                mask_min1(b, T, NT // 2 - 1, 1)
                evac1(T, 1)
                finish1(NT - 1, T, 1)
                dve.wait_ge(x2_rdy, T + 1)
                layer_norm(b, LAYERS + 2, X, H)
                relu(H[:, :, :]).then_inc(h_rdy, 1)
                nc.vector.tensor_tensor(X[:, :, :], X[:, :, :], over_tiles(bo_b[:, :]), ALU.add)
                for src, hi, lo, k in ((HW, qh, ql, 0), (AGG, kh, kl, 1)):
                    dve.wait_ge(qk2_act, b * 8 + 4 * (k + 1))
                    link(b, nc.vector.tensor_copy(hi[:, :], src[:, :]))
                    nc.vector.tensor_tensor(lo[:, :], src[:, :], hi[:, :].bitcast(F32), ALU.subtract
                                            ).then_inc(qk2_dve, 1)
                for g in range(NC):
                    dve.wait_ge(v_ps, b * NC + g + 1)
                    nc.vector.tensor_tensor(
                        V[:, g * TPC:(g + 1) * TPC, :], ps[:, 4 + g, :].rearrange("p (t d) -> p t d", d=D),
                        bv_b[:, :].rearrange("p (o d) -> p o d", o=1).broadcast_to([P, TPC, D]), ALU.add
                    ).then_inc(v_sb, 1)
                dve.wait_ge(st_in, (b + 1) * (16 * 32))
                S0 = b * (NT * HEADS)
                mask_tile2(b, 0, 0, 0)
                for h in range(HEADS):
                    min2(S0 + h, h)
                    if h >= 2:
                        evac2(S0 + h - 2)
                        finish2(0, S0 + h - 2, h - 2)

                def tile2(t, half, u):
                    mask_tile2(b, t, half, u)
                    for h in range(HEADS):
                        s = S0 + t * HEADS + h
                        min2(s, h)
                        evac2(s - 2)
                        finish2(t - 1 if h < 2 else t, s - 2, (h - 2) % HEADS)

                tile2(1, 0, 1)
                with dve.Fori(1, NT // 2) as tt:
                    tile2(tt * 2, tt, 0)
                    tile2(tt * 2 + 1, tt, 1)
                for h in (2, 3):
                    r = NT * HEADS - 4 + h
                    evac2(S0 + r)
                    finish2(NT - 1, S0 + r, h)
                for g in range(NC):
                    dve.wait_ge(x3_ps, b * NC + g + 1)
                    xg = X[:, g * TPC:(g + 1) * TPC, :]
                    last = nc.vector.tensor_tensor(xg, ps[:, 4 + g, :].rearrange("p (t d) -> p t d", d=D), xg, ALU.add)
                link(b, last)
                layer_norm(b, LAYERS + 3, X, H)
                link(b, relu(H[:, :, :]))
                dve.wait_ge(dinv_rdy, b + 1)
                nc.vector.tensor_tensor(H[:, :, :], H[:, :, :],
                                        dinv[:, :].rearrange("p (t o) -> p t o", o=1).broadcast_to([P, NT, D]),
                                        ALU.mult).then_inc(diag_rdy, 1)
                OUT = tiles(HW)
                with dve.Fori(0, NT // 2) as tt:
                    for u in range(2):
                        T = b * NT + tt * 2 + u
                        ring_wait(dve, b, 2, tt, u)
                        blk = ring[:, u, tcols(tt * 2 + u)]
                        nc.vector.tensor_tensor(blk, blk, ident[:, :], ALU.add).then_inc(diag_rdy, 1)
                        AT = (AGG, HT)[u]
                        for g in range(2, 4):
                            dve.wait_ge(at3_ps, T * NC + g + 1)
                            nc.vector.tensor_copy(AT[:, g * CH:(g + 1) * CH], ps[:, (4 * u + g) % 6, :]
                                                  ).then_inc(at3_dve, 1)
                    for u in range(2):
                        T = b * NT + tt * 2 + u
                        dve.wait_ge(o3_ps, T + 1)
                        t1 = bass.ds(tt * 2 + u, 1)
                        nc.vector.scalar_tensor_tensor(
                            out=OUT[:, t1, :].rearrange("p o d -> p (o d)"), in0=ps[:, 6 + u, P:2 * P],
                            scalar=dinv[:, t1], in1=X[:, t1, :].rearrange("p o d -> p (o d)"),
                            op0=ALU.mult, op1=ALU.add).then_inc(o3_rdy, 1)
            assert own.k == own.per_batch, own.k

        @block.tensor
        def _(pe):
            mm = nc.tensor.matmul
            pe.wait_ge(const_in, 16 * CONST_DMAS)
            pe.wait_ge(id_rdy, 1)
            nc.tensor.transpose(ps[:, 0, 0:P], w12[:, :], ident[:, :]).then_inc(w12_ps, 1)
            pe.wait_ge(const_rdy, 1)

            def transposes(src, bank, done):
                for t in range(NT):
                    last = nc.tensor.transpose(ps[:, bank + t // TPC, (t % TPC) * P:(t % TPC + 1) * P], src(t), ident[:, :])
                    if t % TPC == TPC - 1:
                        last.then_inc(done, 1)

            def h_transposes(b, i):
                pe.wait_ge(h_rdy, b * HTS + i + 1)
                transposes(lambda t: H[:, t, :], 0, ht_ps)
                pe.wait_ge(ht_sb, b * (HTS * NC) + (i + 1) * NC)

            def quad(b, T, m, u, first):
                q = T * QUADS + m
                pe.wait_ge(e_dve, q + 1)
                pe.wait_ge(e_act, q + 1)
                if m == 0 and not first:
                    pe.wait_ge(x2_rdy, T - 1)
                s = 4 * (m % 2)
                win = a_win[:, QROWS - 2 - 2 * m:2 * QROWS - 2 - 2 * m]
                for c in range(NC):
                    for grp in range(4):
                        last = mm(ps[QROWS * grp:QROWS * (grp + 1), 4 * u + c, :], win,
                                  E[:, s + grp, c * CH:(c + 1) * CH], start=(m == 0), stop=(m == QUADS - 1),
                                  tile_position=(0, QROWS * grp))
                last.then_inc(e_used, 1)

            def probs_t1(T, u):
                pe.wait_ge(p1_rdy, T + 1)
                transposes(lambda t: T1[:, t * P:(t + 1) * P], 4 * u, pt1_ps)

            def out1(T, u):
                pe.wait_ge(pt1_act, T + 1)
                pe.wait_ge(pt1_dve, T + 1)
                for j in range(NT):
                    last = mm(ps[:, 4 * u, 0:D], PT1[:, j * P:(j + 1) * P], H[:, j, :], start=(j == 0), stop=(j == NT - 1))
                last.then_inc(o1_ps, 1)

            def tile1(b, t, u, tail, first):
                T = b * NT + t
                for m in range(QUADS):
                    quad(b, T, m, u, first)
                    if tail and m == 5:
                        probs_t1(T - 1, 1 - u)
                    if tail and m == 9:
                        out1(T - 1, 1 - u)

            def scores2(s, h, t, b, start):
                if h == 0:
                    pe.wait_ge(qcur_rdy, b * NT + t + 1)
                if not start:
                    pe.wait_ge(t2_rdy, s)
                for c in range(NC):
                    last = mm(ps[:, c, :], qcur[:, h, :], kst[:, h, c * CH:(c + 1) * CH], start=True, stop=True)
                last.then_inc(s2_ps, 1)

            def out2(r, h, start):
                pe.wait_ge(p2_rdy, r + 1)
                if not start:
                    pe.wait_ge(att_rdy, r - 1)

                def tp(g):
                    for k in range(TPC):
                        j = g * TPC + k
                        last = nc.tensor.transpose(ps[:, 4 + g % 2, k * P:(k + 1) * P], T2[:, h, j * P:(j + 1) * P],
                                                   ident[:, :])
                    last.then_inc(pt2_ps, 1)

                def av(g):
                    if g < 2:
                        pe.wait_ge(pt2_act, r * 2 + g + 1)
                    else:
                        pe.wait_ge(pt2_dve, r * 2 + g - 1)
                    for k in range(TPC):
                        j = g * TPC + k
                        last = mm(ps[:, 6 + h % 2, 0:HD], PT2[:, g, k * P:(k + 1) * P],
                                  V[:, j, h * HD:(h + 1) * HD], start=(j == 0), stop=(j == NT - 1))
                    if g == NC - 1:
                        last.then_inc(o2_ps, 1)

                tp(0)
                tp(1)
                av(0)
                tp(2)
                av(1)
                tp(3)
                av(2)
                av(3)

            with pe.Fori(0, NB) as b:
                for l in range(LAYERS):
                    h_transposes(b, l)
                    for t in range(NT):
                        last = mm(ps[:, 4 + t // TPC, (t % TPC) * P:(t % TPC + 1) * P], HT[:, t * P:(t + 1) * P],
                                  w0[:, l, :], start=True, stop=True)
                        if t % TPC == TPC - 1:
                            last.then_inc(hw_ps, 1)
                    pe.wait_ge(hw_sb, b * (LAYERS * NC) + (l + 1) * NC)
                    if l == 0:
                        pe.wait_ge(adj_in, (b + 1) * (16 * NT))
                    for c in range(NC):
                        for t in range(NT):
                            last = mm(ps[:, c, :], HW[:, t * P:(t + 1) * P], A[:, t, c * CH:(c + 1) * CH],
                                      start=(t == 0), stop=(t == NT - 1))
                        last.then_inc(agg_ps, 1)
                    if l == 0:
                        pe.wait_ge(deg_rdy, (b + 1) * NT)
                    pe.wait_ge(agg_sb, b * (LAYERS * NC) + (l + 1) * NC)
                    transposes(lambda t: AGG[:, t * P:(t + 1) * P], 4, z_ps)
                h_transposes(b, LAYERS)
                for c in range(NC):
                    mm(ps[:, 4 + c, :], w1t2[:, :], HT[:, c * CH:(c + 1) * CH], start=True, stop=True).then_inc(qk1_ps, 1)
                pairs = HT[:, :].rearrange("p (g two) -> p g two", two=2)
                for c in range(2):
                    for two in range(2):
                        last = mm(ps[DG * two:DG * (two + 1), c, :], w2t[:, :], pairs[:, c * CH:(c + 1) * CH, two],
                                  start=True, stop=True, tile_position=(0, DG * two))
                    last.then_inc(qk1_ps, 1)
                pe.wait_ge(qk1_sb, (b + 1) * 6)
                tile1(b, 0, 0, False, True)
                tile1(b, 1, 1, True, True)
                with pe.Fori(1, NT // 2) as tt:
                    tile1(b, tt * 2, 0, True, False)
                    tile1(b, tt * 2 + 1, 1, True, False)
                probs_t1(b * NT + NT - 1, 1)
                out1(b * NT + NT - 1, 1)
                h_transposes(b, LAYERS + 1)
                for bank, w in ((4, wq), (0, wk)):
                    for c in range(NC):
                        mm(ps[:, bank + c, :], w[:, :], HT[:, c * CH:(c + 1) * CH], start=True, stop=True).then_inc(qk2_ps, 1)
                pe.wait_ge(qk2_act, b * 8 + 4)
                for t in range(NT):
                    last = mm(ps[:, 4 + t // TPC, (t % TPC) * P:(t % TPC + 1) * P], HT[:, t * P:(t + 1) * P], wv[:, :],
                              start=True, stop=True)
                    if t % TPC == TPC - 1:
                        last.then_inc(v_ps, 1)
                pe.wait_ge(v_sb, (b + 1) * NC)
                pe.wait_ge(qk2_act, (b + 1) * 8)
                pe.wait_ge(st_in, (b + 1) * (16 * 32))
                S0 = b * (NT * HEADS)
                for h in range(HEADS):
                    scores2(S0 + h, h, 0, b, h == 0)
                    if h >= 2:
                        out2(S0 + h - 2, h - 2, True)
                for h in range(HEADS):
                    scores2(S0 + HEADS + h, h, 1, b, False)
                    out2(S0 + HEADS + h - 2, (h - 2) % HEADS, False)
                with pe.Fori(2, NT) as t:
                    for h in range(HEADS):
                        s = S0 + t * HEADS + h
                        scores2(s, h, t, b, False)
                        out2(s - 2, (h - 2) % HEADS, False)
                for h in (2, 3):
                    out2(S0 + NT * HEADS - 4 + h, h, False)
                pe.wait_ge(att_rdy, (b + 1) * (NT * HEADS))
                transposes(lambda t: H[:, t, :], 0, at_ps)
                for t in range(NT):
                    if t % TPC == 0:
                        pe.wait_ge(at_sb, b * NC + t // TPC + 1)
                    last = mm(ps[:, 4 + t // TPC, (t % TPC) * P:(t % TPC + 1) * P], HT[:, t * P:(t + 1) * P], wo[:, :],
                              start=True, stop=True)
                    if t % TPC == TPC - 1:
                        last.then_inc(x3_ps, 1)
                with pe.Fori(0, NT // 2) as tt:
                    for u in range(2):
                        T = b * NT + tt * 2 + u
                        if u:
                            pe.wait_ge(at3_act, T * 2)
                        pe.wait_ge(diag_rdy, b * (NT + 1) + tt * 2 + (u + 2))
                        for j in range(NT):
                            g = j // TPC
                            last = nc.tensor.transpose(ps[:, (4 * u + g) % 6, (j % TPC) * P:(j % TPC + 1) * P],
                                                       ring[:, u, j * P:(j + 1) * P], ident[:, :])
                            if j % TPC == TPC - 1:
                                last.then_inc(at3_ps, 1)
                    for u in range(2):
                        T = b * NT + tt * 2 + u
                        AT = (AGG, HT)[u]
                        pe.wait_ge(at3_act, (T + 1) * 2)
                        pe.wait_ge(at3_dve, (T + 1) * 2)
                        pe.wait_ge(o3_rdy, T + 2)
                        for j in range(NT):
                            last = mm(ps[:, 6 + u, 0:P], H[:, j, :], AT[:, j * P:(j + 1) * P],
                                      start=(j == 0), stop=(j == NT - 1))
                            if j == 0:
                                last.then_inc(ring_free, 1)
                        last.then_inc(hb_ps, 1)
                    for u in range(2):
                        T = b * NT + tt * 2 + u
                        pe.wait_ge(hb_sb, T + 1)
                        mm(ps[:, 6 + u, P:2 * P], hbT[:, u, :], wb[:, :], start=True, stop=True).then_inc(o3_ps, 1)


_INS = ["x", "adj", "L0_gnn_Ws", "L0_gnn_bs", "L0_gnn_gammas", "L0_gnn_betas", "L1_gnn_W1", "L1_gnn_W2", "L1_gnn_a",
        "L2_gnn_Wq", "L2_gnn_bq", "L2_gnn_Wk", "L2_gnn_bk", "L2_gnn_Wv", "L2_gnn_bv", "L2_gnn_Wo", "L2_gnn_bo",
        "L3_gnn_B"]


def kernel(**inputs):
    import numpy as np
    import concourse.bacc as bacc
    from concourse.bass_utils import run_bass_kernel_spmd

    nc = bacc.Bacc("TRN2", target_bir_lowering=False, num_devices=1)
    arrays, args = {}, []
    for name in _INS:
        a = np.ascontiguousarray(inputs[name])
        arrays[f"in_{name}"] = a
        args.append(nc.dram_tensor(f"in_{name}", a.shape, mybir.dt.from_np(a.dtype), kind="ExternalInput").ap())
    args.append(nc.dram_tensor("out_x", (NB, N, D), F32, kind="ExternalOutput").ap())
    build(nc, *args)
    r = run_bass_kernel_spmd(nc, [arrays], core_ids=[0])
    return r.results[0]["out_x"]
```

```python
from contextlib import ExitStack

import concourse.bass as bass
from concourse import mybir

F32 = mybir.dt.float32
F32R = mybir.dt.float32r
ALU = mybir.AluOpType
ACT = mybir.ActivationFunctionType

P = 128
NB, N, D = 8, 2048, 128
NT = N // P
CH = 512
NC = N // CH
TPC = NT // NC
LAYERS = 3
HEADS, HD = 4, 32
DG = 64
QUADS = 16
QROWS = P // 4
LN_EPS = 1e-5
BIG = 3.0e38
MASK_ADD = 1e22
MASK_DOT = 1e9
SCALE = float(1.0 / (HD ** 0.5))
LNS = LAYERS + 4
HTS = LAYERS + 2
STEPS = NT * HEADS


EQ = 3
TURN = QUADS + QUADS // 2


def e_slot(u, m):
    return 4 * ((u * QUADS + m - TURN) % (2 * QUADS) % EQ)


def e_lag(u, m):
    return 2 if u * QUADS + m - TURN in (0, 1) else EQ


class Steps:

    def __init__(self, sem, per_batch):
        self.sem, self.per_batch, self.k = sem, per_batch, 0

    def done(self, ins):
        self.k += 1
        ins.then_inc(self.sem, 1)

    def wait(self, eng, b):
        eng.wait_ge(self.sem, b * self.per_batch + self.k)


def build(nc, x, adj, Ws, bs, gammas, betas, W1, W2, a_vec, Wq, bq, Wk, bk, Wv, bv, Wo, bo, Bw, out):
    x_v = x.rearrange("b (t p) d -> b p t d", p=P)
    out_v = out.rearrange("b (t p) d -> b p t d", p=P)
    adj_v = adj.rearrange("b (t p) n -> b t p n", p=P)

    with ExitStack() as ctx:
        def sb(name, shape, dt=F32, where=None):
            return (where or ctx).enter_context(nc.sbuf_tensor(name, shape, dt))

        def sem(name):
            return ctx.enter_context(nc.semaphore(name))

        ring = sb("adj_ring", [P, 2, N])
        X = sb("X", [P, NT, D])
        H = sb("H", [P, NT, D])
        HT = sb("HT", [P, N])
        HW = sb("HW", [P, N])
        AGG = sb("AGG", [P, N])
        ident = sb("ident", [P, P])
        w0 = sb("w0", [P, LAYERS, D])
        b0 = sb("b0", [P, LAYERS])
        gam = sb("gam", [P, LAYERS, D])
        bet = sb("bet", [P, LAYERS, D])
        w12 = sb("w12", [P, D])
        w1t2 = sb("w1t2", [P, P])
        w2t = sb("w2t", [P, DG])
        a_col = sb("a_col", [P, 1])
        a_win = sb("a_win", [P, 2 * QROWS - 2])
        wq = sb("wq", [P, D])
        wk = sb("wk", [P, D])
        wv = sb("wv", [P, D])
        wo = sb("wo", [P, D])
        wb = sb("wb", [P, D])
        bq_c = sb("bq_c", [P, 1])
        bqs_c = sb("bqs_c", [P, 1])
        bk_c = sb("bk_c", [P, 1])
        bv_b = sb("bv_b", [P, D])
        bo_b = sb("bo_b", [P, D])
        halves = sb("halves", [P, NT])
        epses = sb("epses", [P, NT])
        ones = sb("ones", [P, NT])
        stats = sb("stats", [P, NT, 6])
        mv = sb("mv", [P, NT, 2])
        var = sb("var", [P, NT])
        rstd = sb("rstd", [P, NT])
        deg = sb("deg", [P, NT])
        deg1 = sb("deg1", [P, NT])
        dinv = sb("dinv", [P, NT])
        kd = sb("kd", [P, 2, 64])
        ka = sb("ka", [P, 2, 64])
        nmin1 = sb("nmin1", [P, 2])
        rsum1 = sb("rsum1", [P, 2])
        rinv1 = sb("rinv1", [P, 2])
        nmin2 = sb("nmin2", [P, HEADS])
        rsum2 = sb("rsum2", [P, HEADS])
        rinv2 = sb("rinv2", [P, HEADS])
        qcur = sb("qcur", [P, 2, HEADS, P], F32R)
        sel = sb("sel", [P, HD])
        o4 = sb("o4", [P, 2, P])
        hbT = sb("hbT", [P, 2, P])

        with ExitStack() as ph:
            A = sb("adj_res", [P, NT, N], where=ph)
        with ExitStack() as ph:
            E = sb("E", [P, 4 * EQ, N], where=ph)
            Q2 = sb("Q2", [P, N], where=ph)
            K2 = sb("K2", [P, N // 2], where=ph)
            T1 = sb("T1", [P, N], where=ph)
            PT1 = sb("PT1", [P, N], where=ph)
        with ExitStack() as ph:
            kst = sb("kst", [P, HEADS, N], F32R, where=ph)
            qst = sb("qst", [P, HEADS, N], F32R, where=ph)
            V = sb("V", [P, NT, D], where=ph)
            PT2 = sb("PT2", [P, NC, CH], where=ph)
            with ExitStack() as sub:
                T2 = sb("T2", [P, HEADS, N], where=sub)
            with ExitStack() as sub:
                qh = sb("qh", [P, N], F32R, where=sub)
                ql = sb("ql", [P, N], F32R, where=sub)
                kh = sb("kh", [P, N], F32R, where=sub)
                kl = sb("kl", [P, N], F32R, where=sub)

        ps = ctx.enter_context(nc.psum_tensor("ps", [P, 8, CH], F32))

        waited = sem("waited")
        mask2_rdy = sem("mask2_rdy")
        const_in = sem("const_in")
        const_w = sem("const_w")
        w12_ps = sem("w12_ps")
        const_rdy = sem("const_rdy")
        id_rdy = sem("id_rdy")
        x_in = sem("x_in")
        adj_in = sem("adj_in")
        ring_in = [sem("ring_in0"), sem("ring_in1")]
        ring_free = sem("ring_free")
        dve_self = sem("dve_self")
        pool_self = sem("pool_self")
        ln_stats = sem("ln_stats")
        ln_rstd = sem("ln_rstd")
        deg_rdy = sem("deg_rdy")
        dinv_rdy = sem("dinv_rdy")
        h_rdy = sem("h_rdy")
        ht_ps = sem("ht_ps")
        ht_sb = sem("ht_sb")
        hw_ps = sem("hw_ps")
        hw_sb = sem("hw_sb")
        agg_ps = sem("agg_ps")
        agg_sb = sem("agg_sb")
        z_ps = sem("z_ps")
        qk1_ps = sem("qk1_ps")
        qk1_sb = sem("qk1_sb")
        kd_rdy = sem("kd_rdy")
        ka_rdy = sem("ka_rdy")
        e_dve = sem("e_dve")
        e_act = sem("e_act")
        e_used = sem("e_used")
        mask1 = sem("mask1")
        t1_rdy = sem("t1_rdy")
        p1_rdy = sem("p1_rdy")
        pt1_ps = sem("pt1_ps")
        pt1_act = sem("pt1_act")
        pt1_dve = sem("pt1_dve")
        rinv1_rdy = sem("rinv1_rdy")
        o1_ps = sem("o1_ps")
        x2_rdy = sem("x2_rdy")
        qk2_ps = sem("qk2_ps")
        qk2_act = sem("qk2_act")
        qk2_dve = sem("qk2_dve")
        v_ps = sem("v_ps")
        v_sb = sem("v_sb")
        st_in = sem("st_in")
        qcur_rdy = sem("qcur_rdy")
        s2_ps = sem("s2_ps")
        t2_rdy = sem("t2_rdy")
        p2_rdy = sem("p2_rdy")
        pt2_ps = sem("pt2_ps")
        pt2_act = sem("pt2_act")
        pt2_dve = sem("pt2_dve")
        rinv2_rdy = sem("rinv2_rdy")
        o2_ps = sem("o2_ps")
        o4_rdy = sem("o4_rdy")
        c2_ps = sem("c2_ps")
        att_rdy = sem("att_rdy")
        at_ps = sem("at_ps")
        at_sb = sem("at_sb")
        x3_ps = sem("x3_ps")
        diag_rdy = sem("diag_rdy")
        at3_ps = sem("at3_ps")
        at3_act = sem("at3_act")
        at3_dve = sem("at3_dve")
        hb_ps = sem("hb_ps")
        hb_sb = sem("hb_sb")
        o3_ps = sem("o3_ps")
        o3_rdy = sem("o3_rdy")
        out_done = sem("out_done")

        CONST_DMAS = 16
        block = ctx.enter_context(nc.Block())

        def alone(eng):
            eng.sem_inc(waited, 1)

        def tcols(t):
            return bass.ds(t * P, P)

        @block.sync
        def _(sp):
            def const(dst, src):
                sp.dma_start(dst, src).then_inc(const_in, 16)

            def bcast(src, n):
                return src.rearrange("(o e) -> o e", o=1).broadcast_to([P, n])

            const(w0[:, :, :], Ws.rearrange("l d e -> d l e"))
            with nc.allow_non_contiguous_dma(reason="one small load"):
                const(b0[:, :], bs.rearrange("l e -> e l"))
            const(gam[:, :, :].rearrange("p l e -> p (l e)"), bcast(gammas.rearrange("l e -> (l e)"), LAYERS * D))
            const(bet[:, :, :].rearrange("p l e -> p (l e)"), bcast(betas.rearrange("l e -> (l e)"), LAYERS * D))
            const(w12[0:DG, :], W1)
            const(w12[DG:P, :], W2)
            const(a_col[0:DG, :], a_vec.rearrange("(e o) -> e o", o=1))
            const(a_col[DG:P, :], a_vec.rearrange("(e o) -> e o", o=1))
            for dst, src in ((wq, Wq), (wk, Wk), (wv, Wv), (wo, Wo), (wb, Bw)):
                const(dst[:, :], src)
            const(bq_c[:, :], bq.rearrange("(e o) -> e o", o=1))
            const(bk_c[:, :], bk.rearrange("(e o) -> e o", o=1))
            const(bo_b[:, :], bcast(bo, D))
            sp.dma_start(bv_b[:, :], bcast(bv, D)).then_inc(out_done, 16)
            with sp.Fori(0, NB) as b:
                sp.wait_ge(o3_rdy, b * NT + 3)
                for t in range(NT):
                    sp.dma_start(X[:, t, :], x_v[bass.ds(b, 1), :, t].rearrange("o p d -> p (o d)")).then_inc(x_in, 16)
                for phase in range(3):
                    with sp.Fori(0, NT // 2) as tt:
                        for u in range(2):
                            sp.wait_ge(ring_free, b * (3 * NT) + tt * 2 + (phase * NT + u + 1))
                            sp.dma_start(ring[:, u, :],
                                         adj_v[bass.ds(b, 1), bass.ds(tt * 2 + u, 1)].rearrange("o c p n -> p (o c n)")
                                         ).then_inc(ring_in[u], 16)
                sp.wait_ge(o3_rdy, b * NT + (NT + 3))
                sp.dma_start(out_v[bass.ds(b, 1)].rearrange("o p t d -> p (o t) d"),
                             HW[:, :].rearrange("p (t d) -> p t d", t=NT)).then_inc(out_done, 16)
            sp.wait_ge(out_done, 16 * (NB + 1))

        def ring_wait(eng, b, phase, half, u):
            eng.wait_ge(ring_in[u], b * (16 * 24) + half * 16 + 16 * (phase * 8 + 1))

        @block.gpsimd
        def _(pool):
            pool.memset(ident[:, :], 0.0).then_inc(pool_self, 1)
            pool.memset(halves[:, :], -0.5).then_inc(pool_self, 1)
            pool.memset(epses[:, :], LN_EPS).then_inc(pool_self, 1)
            pool.memset(ones[:, :], 1.0).then_inc(pool_self, 1)
            pool.wait_ge(pool_self, 4)
            pool.affine_select(out=ident[:, :], in_=ident[:, :], compare_op=ALU.not_equal, fill=1.0, base=0,
                               pattern=[[-1, P]], channel_multiplier=1).then_inc(id_rdy, 1)
            own = Steps(pool_self, LNS + 1)
            own.k = 4

            def rstd_step(b, i):
                pool.wait_ge(ln_stats, b * LNS + i + 1)
                own.done(pool.tensor_tensor(var[:, :], mv[:, :, 1], epses[:, :], ALU.add))
                own.wait(pool, b)
                pool.tensor_tensor(rstd[:, :], var[:, :], halves[:, :], ALU.pow).then_inc(ln_rstd, 1)

            with pool.Fori(0, NB) as b:
                own.k = 4
                for t in range(NT):
                    pool.dma_start(A[:, t, :], adj_v[bass.ds(b, 1), t].rearrange("o p n -> p (o n)")).then_inc(adj_in, 16)
                rstd_step(b, 0)
                pool.wait_ge(deg_rdy, (b + 1) * NT)
                own.done(pool.tensor_tensor(deg1[:, :], deg[:, :], ones[:, :], ALU.add))
                own.wait(pool, b)
                pool.tensor_tensor(dinv[:, :], deg1[:, :], halves[:, :], ALU.pow).then_inc(dinv_rdy, 1)
                for i in range(1, LNS):
                    rstd_step(b, i)

        @block.scalar
        def _(act):
            def evac(dst, src):
                return nc.scalar.activation(dst, src, ACT.Copy)

            def evac_ht(b, i):
                for c in range(NC):
                    act.wait_ge(ht_ps, b * (HTS * NC) + i * NC + c + 1)
                    evac(HT[:, c * CH:(c + 1) * CH], ps[:, c, :]).then_inc(ht_sb, 1)

            def keys(t, T, u, first):
                if not first:
                    act.wait_ge(e_act, (T - 1) * QUADS)
                evac(ka[:, u, :], K2[:, bass.ds(t * 64, 64)]).then_inc(ka_rdy, 1)
                act.wait_ge(ka_rdy, T + 1)

            def quad(T, m, u, first):
                if not (first and m < EQ):
                    act.wait_ge(e_used, T * QUADS + (m - e_lag(u, m) + 1))
                s = e_slot(u, m)
                nc.scalar.activation(E[:, s + 2, N // 2:N], Q2[:, N // 2:N], ACT.Relu, bias=ka[:, u, 32 + m:33 + m])
                nc.scalar.activation(E[:, s + 3, :], Q2[:, :], ACT.Relu, bias=ka[:, u, 48 + m:49 + m]).then_inc(e_act, 1)

            def exp1(T, u):
                act.wait_ge(t1_rdy, T + 1)
                nc.scalar.activation(T1[:, :], T1[:, :], ACT.Exp, bias=nmin1[:, u:u + 1], scale=-1.0,
                                     accum_out=rsum1[:, u:u + 1]).then_inc(p1_rdy, 1)

            def evac1(T, u):
                for g in range(2):
                    act.wait_ge(pt1_ps, T * NC + g + 1)
                    last = evac(PT1[:, g * CH:(g + 1) * CH], ps[:, 4 * u + g, :])
                last.then_inc(pt1_act, 1)

            def tile1(b, t, u, tail, first):
                T = b * NT + t
                keys(t, T, u, first)
                for m in range(QUADS):
                    quad(T, m, u, not tail)
                    if tail and m == 4:
                        exp1(T - 1, 1 - u)
                    if tail and m == 7:
                        evac1(T - 1, 1 - u)

            def exp2(s, h):
                act.wait_ge(t2_rdy, s + 1)
                nc.scalar.activation(T2[:, h, :], T2[:, h, :], ACT.Exp, bias=nmin2[:, h:h + 1], scale=-1.0,
                                     accum_out=rsum2[:, h:h + 1]).then_inc(p2_rdy, 1)

            def norm2(t, r, h):
                act.wait_ge(rinv2_rdy, r + 1)
                act.wait_ge(c2_ps, r + 1)
                dst = H[:, bass.ds(t, 1), h * HD:(h + 1) * HD].rearrange("p o d -> p (o d)")
                nc.scalar.activation(dst, ps[:, 6 + h % 2, P:P + HD], ACT.Copy, scale=rinv2[:, h:h + 1]
                                     ).then_inc(att_rdy, 1)

            def evac2(r):
                for g in range(3):
                    act.wait_ge(pt2_ps, r * NC + g + 1)
                    evac(PT2[:, g, :], ps[:, 4 + g % 2, :]).then_inc(pt2_act, 1)

            def step2(s, t, h, loc=None):
                def there(lag):
                    return loc is None or 0 <= loc - lag < STEPS

                if there(1):
                    exp2(s - 1, (h - 1) % HEADS)
                if there(4):
                    norm2(t - 1, s - 4, h)
                if there(2):
                    evac2(s - 2)

            act.wait_ge(const_rdy, 1)
            with act.Fori(0, NB) as b:
                act.wait_ge(out_done, b * 16 + 16)
                for l in range(LAYERS):
                    evac_ht(b, l)
                    for g in range(NC):
                        act.wait_ge(hw_ps, b * (LAYERS * NC) + l * NC + g + 1)
                        evac(HW[:, g * CH:(g + 1) * CH], ps[:, 4 + g, :]).then_inc(hw_sb, 1)
                    if l == 0:
                        act.wait_ge(adj_in, (b + 1) * (16 * NT))
                        act.wait_ge(hw_sb, b * (LAYERS * NC) + NC)
                        for t in range(NT):
                            nc.scalar.activation(ps[:, 4:8, :].rearrange("p c n -> p (c n)"), A[:, t, :], ACT.Copy,
                                                 accum_out=deg[:, t:t + 1]).then_inc(deg_rdy, 1)
                            act.wait_ge(deg_rdy, b * NT + t + 1)
                    for c in range(NC):
                        act.wait_ge(agg_ps, b * (LAYERS * NC) + l * NC + c + 1)
                        nc.scalar.activation(AGG[:, c * CH:(c + 1) * CH], ps[:, c, :], ACT.Identity,
                                             bias=b0[:, l:l + 1]).then_inc(agg_sb, 1)
                evac_ht(b, LAYERS)
                for c in range(NC):
                    act.wait_ge(qk1_ps, b * 6 + c + 1)
                    evac(Q2[:, c * CH:(c + 1) * CH], ps[:, 4 + c, :]).then_inc(qk1_sb, 1)
                for c in range(2):
                    act.wait_ge(qk1_ps, b * 6 + 4 + c + 1)
                    evac(K2[:, c * CH:(c + 1) * CH], ps[:, c, :]).then_inc(qk1_sb, 1)
                act.wait_ge(qk1_sb, (b + 1) * 6)
                tile1(b, 0, 0, False, True)
                tile1(b, 1, 1, True, True)
                with act.Fori(1, NT // 2) as tt:
                    tile1(b, tt * 2, 0, True, False)
                    tile1(b, tt * 2 + 1, 1, True, False)
                exp1(b * NT + NT - 1, 1)
                evac1(b * NT + NT - 1, 1)
                evac_ht(b, LAYERS + 1)
                for c in range(NC):
                    act.wait_ge(qk2_ps, b * 8 + c + 1)
                    nc.scalar.activation(HW[:, c * CH:(c + 1) * CH], ps[:, 4 + c, :], ACT.Identity,
                                         bias=bqs_c[:, 0:1], scale=-SCALE).then_inc(qk2_act, 1)
                for c in range(NC):
                    act.wait_ge(qk2_ps, b * 8 + 4 + c + 1)
                    nc.scalar.activation(AGG[:, c * CH:(c + 1) * CH], ps[:, c, :], ACT.Identity,
                                         bias=bk_c[:, 0:1]).then_inc(qk2_act, 1)
                for dst, parts, k in ((qst, (qh, qh, ql, ql), 1), (kst, (kh, kl, kh, kl), 2)):
                    act.wait_ge(qk2_dve, b * 2 + k)
                    for h in range(HEADS):
                        for blk in range(4):
                            act.dma_start(dst[HD * blk:HD * (blk + 1), h, :].bitcast(F32),
                                          parts[blk][HD * h:HD * (h + 1), :].bitcast(F32)).then_inc(st_in, 16)
                S0 = b * (NT * HEADS)
                for loc in range(HEADS):
                    step2(S0 + loc, 0, loc, loc)
                with act.Fori(1, NT) as t:
                    for h in range(HEADS):
                        step2(S0 + t * HEADS + h, t, h)
                for loc in range(STEPS, STEPS + 4):
                    step2(S0 + loc, NT, loc % HEADS, loc)
                for c in range(NC):
                    act.wait_ge(at_ps, b * NC + c + 1)
                    evac(HT[:, c * CH:(c + 1) * CH], ps[:, c, :]).then_inc(at_sb, 1)
                with act.Fori(0, NT // 2) as tt:
                    for u in range(2):
                        T = b * NT + tt * 2 + u
                        AT = (AGG, HT)[u]
                        for g in range(2):
                            act.wait_ge(at3_ps, T * NC + g + 1)
                            evac(AT[:, g * CH:(g + 1) * CH], ps[:, (4 * u + g) % 6, :]).then_inc(at3_act, 1)
                    for u in range(2):
                        T = b * NT + tt * 2 + u
                        act.wait_ge(hb_ps, T + 1)
                        evac(hbT[:, u, :], ps[:, 6 + u, 0:P]).then_inc(hb_sb, 1)

        @block.vector
        def _(dve):
            own = Steps(dve_self, 4 * LNS + 1)

            def link(b, ins):
                own.done(ins)
                own.wait(dve, b)

            nc.vector.memset(a_win[:, :], 0.0).then_inc(ring_free, 1)
            nc.vector.memset(mv[:, :, :], 0.0).then_inc(ring_free, 1)
            for buf in (stats[:, :, :], dinv[:, :], rstd[:, :]):
                nc.vector.memset(buf, 0.0).then_inc(o3_rdy, 1)
            dve.wait_ge(ring_free, 2)
            dve.wait_ge(o3_rdy, 3)
            dve.wait_ge(out_done, 16)
            dve.wait_ge(const_in, 16 * CONST_DMAS)
            nc.vector.tensor_scalar(a_win[0:DG, QROWS - 2:QROWS - 1], a_col[0:DG, :], -1.0, None, ALU.mult)
            nc.vector.tensor_scalar(a_win[DG:P, QROWS - 1:QROWS], a_col[DG:P, :], -1.0, None, ALU.mult)
            nc.vector.tensor_scalar(bqs_c[:, :], bq_c[:, :], -SCALE, None, ALU.mult)
            dve.wait_ge(id_rdy, 1)
            for k in range(P // HD):
                nc.vector.tensor_copy(sel[HD * k:HD * (k + 1), :], ident[HD * k:HD * (k + 1), HD * k:HD * (k + 1)])
            dve.wait_ge(w12_ps, 1)
            nc.vector.tensor_copy(w1t2[:, 0:DG], ps[:, 0, 0:DG])
            nc.vector.tensor_copy(w1t2[:, DG:P], ps[:, 0, 0:DG])
            nc.vector.tensor_copy(w2t[:, :], ps[:, 0, DG:P]).then_inc(const_rdy, 1)

            def layer_norm(b, i, src, dst):
                for t in range(NT):
                    last = nc.vector.bn_stats(stats[:, t, :], src[:, t, :])
                link(b, last)
                alone(dve)
                for t in range(NT):
                    last = nc.vector.bn_aggr(mv[:, t, :], stats[:, t, :])
                last.then_inc(ln_stats, 1)
                dve.wait_ge(ln_rstd, b * LNS + i + 1)
                for t in range(NT):
                    last = nc.vector.tensor_scalar(dst[:, t, :], src[:, t, :], mv[:, t, 0:1], rstd[:, t:t + 1],
                                                   ALU.subtract, ALU.mult)
                link(b, last)

            def relu(dst):
                return nc.vector.tensor_scalar(dst, dst, 0.0, None, ALU.max)

            def tiles(buf):
                return buf[:, :].rearrange("p (t d) -> p t d", t=NT)

            def over_tiles(row):
                return row.rearrange("p (o d) -> p o d", o=1).broadcast_to([P, NT, D])

            def keys(t, T, u, first):
                if not first:
                    dve.wait_ge(e_dve, (T - 1) * QUADS)
                nc.vector.tensor_copy(kd[:, u, :], K2[:, bass.ds(t * 64, 64)]).then_inc(kd_rdy, 1)
                dve.wait_ge(kd_rdy, T + 1)

            def quad(T, m, u, first):
                if not (first and m < EQ):
                    dve.wait_ge(e_used, T * QUADS + (m - e_lag(u, m) + 1))
                s = e_slot(u, m)
                nc.vector.tensor_scalar(E[:, s, :], Q2[:, :], kd[:, u, m:m + 1], 0.0, ALU.add, ALU.max)
                nc.vector.tensor_scalar(E[:, s + 1, :], Q2[:, :], kd[:, u, 16 + m:17 + m], 0.0, ALU.add, ALU.max)
                nc.vector.tensor_scalar(E[:, s + 2, 0:N // 2], Q2[:, 0:N // 2], kd[:, u, 32 + m:33 + m], 0.0,
                                        ALU.add, ALU.max).then_inc(e_dve, 1)

            def mask1_tile(b, half, u):
                ring_wait(dve, b, 0, half, u)
                nc.vector.tensor_scalar(ring[:, u, :], ring[:, u, :], 0.0, MASK_ADD, ALU.is_le, ALU.mult
                                        ).then_inc(mask1, 1)

            def min1(T, u):
                dve.wait_ge(e_used, (T + 1) * QUADS)
                dve.wait_ge(mask1, T + 1)
                alone(dve)
                nc.vector.tensor_tensor_reduce(
                    out=T1[:, :], in0=ps[:, 4 * u:4 * u + 4, :].rearrange("p c n -> p (c n)"), in1=ring[:, u, :],
                    scale=1.0, scalar=BIG, op0=ALU.add, op1=ALU.min, accum_out=nmin1[:, u:u + 1]
                ).then_inc(t1_rdy, 1)
                dve.wait_ge(t1_rdy, T + 1)
                dve.sem_inc(ring_free, 1)

            def evac1(T, u):
                for g in range(2, 4):
                    dve.wait_ge(pt1_ps, T * NC + g + 1)
                    last = nc.vector.tensor_copy(PT1[:, g * CH:(g + 1) * CH], ps[:, 4 * u + g, :])
                last.then_inc(pt1_dve, 1)

            def finish1(t, T, u):
                dve.wait_ge(p1_rdy, T + 1)
                nc.vector.reciprocal(rinv1[:, u:u + 1], rsum1[:, u:u + 1]).then_inc(rinv1_rdy, 1)
                dve.wait_ge(rinv1_rdy, T + 1)
                dve.wait_ge(o1_ps, T + 1)
                xt = X[:, bass.ds(t, 1), :].rearrange("p o d -> p (o d)")
                nc.vector.scalar_tensor_tensor(out=xt, in0=ps[:, 4 * u, 0:D], scalar=rinv1[:, u:u + 1], in1=xt,
                                               op0=ALU.mult, op1=ALU.add).then_inc(x2_rdy, 1)

            def tile1(b, t, u, tail, half, first):
                T = b * NT + t
                keys(t, T, u, first)
                for m in range(QUADS):
                    quad(T, m, u, not tail)
                    if tail and m == 2:
                        min1(T - 1, 1 - u)
                    if tail and m == 7:
                        evac1(T - 1, 1 - u)
                    if tail and m == 11:
                        finish1(t - 1, T - 1, 1 - u)
                    if m == 13:
                        mask1_tile(b, half, u)

            def queries2(b, t, u):
                nc.vector.tensor_copy(qcur[:, u, :, :], qst[:, :, tcols(t)].bitcast(F32)).then_inc(qcur_rdy, 1)

            def mask2(b, t, half, u):
                ring_wait(dve, b, 1, half, u)
                nc.vector.tensor_scalar(ring[:, u, :], ring[:, u, :], 1.0, -MASK_DOT, ALU.subtract, ALU.mult
                                        ).then_inc(mask2_rdy, 1)

            def min2(s, h, u):
                dve.wait_ge(s2_ps, s + 1)
                alone(dve)
                nc.vector.tensor_tensor_reduce(
                    out=T2[:, h, :], in0=ps[:, 0:4, :].rearrange("p c n -> p (c n)"), in1=ring[:, u, :],
                    scale=1.0, scalar=BIG, op0=ALU.add, op1=ALU.min, accum_out=nmin2[:, h:h + 1]
                ).then_inc(t2_rdy, 1)

            def evac2(r):
                dve.wait_ge(pt2_ps, (r + 1) * NC)
                nc.vector.tensor_copy(PT2[:, NC - 1, :], ps[:, 4 + (NC - 1) % 2, :]).then_inc(pt2_dve, 1)

            def partial2(r, h):
                dve.wait_ge(p2_rdy, r + 1)
                nc.vector.reciprocal(rinv2[:, h:h + 1], rsum2[:, h:h + 1]).then_inc(rinv2_rdy, 1)
                dve.wait_ge(o2_ps, r + 1)
                nc.vector.tensor_copy(o4[:, h % 2, :], ps[:, 6 + h % 2, 0:P]).then_inc(o4_rdy, 1)

            def step2(b, s, t, h, u, loc=None, last=False, half=0):
                def there(lag):
                    return loc is None or 0 <= loc - lag < STEPS

                if there(4):
                    partial2(s - 4, h)
                if there(3):
                    evac2(s - 3)
                if there(0):
                    if h == 0:
                        dve.wait_ge(mask2_rdy, b * NT + t + 1)
                    min2(s, h, u)
                    if h == 1 and not last:
                        queries2(b, t + 1, 1 - u)
                    if h == 2 and not last:
                        mask2(b, t + 1, half, 1 - u)
                    if h == 3:
                        dve.wait_ge(t2_rdy, s + 1)
                        dve.sem_inc(ring_free, 1)

            own.k = 0
            with dve.Fori(0, NB) as b:
                dve.wait_ge(x_in, (b + 1) * (16 * NT))
                layer_norm(b, 0, X, H)
                relu(H[:, :, :]).then_inc(h_rdy, 1)
                for l in range(LAYERS):
                    Z = tiles(HT)
                    for g in range(NC):
                        dve.wait_ge(z_ps, b * (LAYERS * NC) + l * NC + g + 1)
                        last = nc.vector.tensor_tensor(
                            Z[:, g * TPC:(g + 1) * TPC, :],
                            ps[:, 4 + g, :].rearrange("p (t d) -> p t d", d=D),
                            H[:, g * TPC:(g + 1) * TPC, :], ALU.add)
                    link(b, last)
                    layer_norm(b, l + 1, Z, Z)
                    link(b, nc.vector.tensor_tensor(Z, Z, over_tiles(gam[:, l, :]), ALU.mult))
                    link(b, nc.vector.tensor_tensor(Z, Z, over_tiles(bet[:, l, :]), ALU.add))
                    last = nc.vector.tensor_scalar(H[:, :, :], Z, 0.0, None, ALU.max)
                    if l < LAYERS - 1:
                        last.then_inc(h_rdy, 1)
                        dve.wait_ge(h_rdy, b * HTS + l + 2)
                link(b, last)
                link(b, nc.vector.tensor_tensor(X[:, :, :], X[:, :, :], H[:, :, :], ALU.add))
                layer_norm(b, LAYERS + 1, X, H)
                relu(H[:, :, :]).then_inc(h_rdy, 1)
                dve.wait_ge(qk1_sb, (b + 1) * 6)
                tile1(b, 0, 0, False, 0, True)
                tile1(b, 1, 1, True, 0, True)
                with dve.Fori(1, NT // 2) as tt:
                    tile1(b, tt * 2, 0, True, tt, False)
                    tile1(b, tt * 2 + 1, 1, True, tt, False)
                T = b * NT + NT - 1
                min1(T, 1)
                evac1(T, 1)
                finish1(NT - 1, T, 1)
                dve.wait_ge(x2_rdy, T + 1)
                layer_norm(b, LAYERS + 2, X, H)
                relu(H[:, :, :]).then_inc(h_rdy, 1)
                nc.vector.tensor_tensor(X[:, :, :], X[:, :, :], over_tiles(bo_b[:, :]), ALU.add)
                for src, hi, lo, k in ((HW, qh, ql, 0), (AGG, kh, kl, 1)):
                    dve.wait_ge(qk2_act, b * 8 + 4 * (k + 1))
                    link(b, nc.vector.tensor_copy(hi[:, :], src[:, :]))
                    nc.vector.tensor_tensor(lo[:, :], src[:, :], hi[:, :].bitcast(F32), ALU.subtract
                                            ).then_inc(qk2_dve, 1)
                for g in range(NC):
                    dve.wait_ge(v_ps, b * NC + g + 1)
                    nc.vector.tensor_tensor(
                        V[:, g * TPC:(g + 1) * TPC, :], ps[:, 4 + g, :].rearrange("p (t d) -> p t d", d=D),
                        bv_b[:, :].rearrange("p (o d) -> p o d", o=1).broadcast_to([P, TPC, D]), ALU.add
                    ).then_inc(v_sb, 1)
                dve.wait_ge(st_in, (b + 1) * (16 * 32))
                S0 = b * (NT * HEADS)
                queries2(b, 0, 0)
                mask2(b, 0, 0, 0)
                for loc in range(HEADS):
                    step2(b, S0 + loc, 0, loc, 0, loc)
                for h in range(HEADS):
                    step2(b, S0 + HEADS + h, 1, h, 1, half=1)
                with dve.Fori(1, NT // 2 - 1) as tt:
                    for u in range(2):
                        for h in range(HEADS):
                            step2(b, S0 + tt * (2 * HEADS) + (HEADS * u + h), tt * 2 + u, h, u, half=tt + u)
                for t in (NT - 2, NT - 1):
                    for h in range(HEADS):
                        step2(b, S0 + t * HEADS + h, t, h, t % 2, last=(t == NT - 1), half=NT // 2 - 1)
                for loc in range(STEPS, STEPS + 4):
                    step2(b, S0 + loc, NT, loc % HEADS, 0, loc)
                for g in range(NC):
                    dve.wait_ge(x3_ps, b * NC + g + 1)
                    xg = X[:, g * TPC:(g + 1) * TPC, :]
                    last = nc.vector.tensor_tensor(xg, ps[:, 4 + g, :].rearrange("p (t d) -> p t d", d=D), xg, ALU.add)
                link(b, last)
                layer_norm(b, LAYERS + 3, X, H)
                link(b, relu(H[:, :, :]))
                dve.wait_ge(dinv_rdy, b + 1)
                nc.vector.tensor_tensor(H[:, :, :], H[:, :, :],
                                        dinv[:, :].rearrange("p (t o) -> p t o", o=1).broadcast_to([P, NT, D]),
                                        ALU.mult).then_inc(diag_rdy, 1)
                OUT = tiles(HW)
                with dve.Fori(0, NT // 2) as tt:
                    for u in range(2):
                        T = b * NT + tt * 2 + u
                        ring_wait(dve, b, 2, tt, u)
                        blk = ring[:, u, tcols(tt * 2 + u)]
                        nc.vector.tensor_tensor(blk, blk, ident[:, :], ALU.add).then_inc(diag_rdy, 1)
                        AT = (AGG, HT)[u]
                        for g in range(2, 4):
                            dve.wait_ge(at3_ps, T * NC + g + 1)
                            nc.vector.tensor_copy(AT[:, g * CH:(g + 1) * CH], ps[:, (4 * u + g) % 6, :]
                                                  ).then_inc(at3_dve, 1)
                    for u in range(2):
                        T = b * NT + tt * 2 + u
                        dve.wait_ge(o3_ps, T + 1)
                        t1 = bass.ds(tt * 2 + u, 1)
                        nc.vector.scalar_tensor_tensor(
                            out=OUT[:, t1, :].rearrange("p o d -> p (o d)"), in0=ps[:, 6 + u, P:2 * P],
                            scalar=dinv[:, t1], in1=X[:, t1, :].rearrange("p o d -> p (o d)"),
                            op0=ALU.mult, op1=ALU.add).then_inc(o3_rdy, 1)
            assert own.k == own.per_batch, own.k

        @block.tensor
        def _(pe):
            mm = nc.tensor.matmul
            pe.wait_ge(const_in, 16 * CONST_DMAS)
            pe.wait_ge(id_rdy, 1)
            nc.tensor.transpose(ps[:, 0, 0:P], w12[:, :], ident[:, :]).then_inc(w12_ps, 1)
            pe.wait_ge(const_rdy, 1)

            def transposes(src, bank, done):
                for t in range(NT):
                    last = nc.tensor.transpose(ps[:, bank + t // TPC, (t % TPC) * P:(t % TPC + 1) * P], src(t), ident[:, :])
                    if t % TPC == TPC - 1:
                        last.then_inc(done, 1)

            def h_transposes(b, i):
                pe.wait_ge(h_rdy, b * HTS + i + 1)
                transposes(lambda t: H[:, t, :], 0, ht_ps)
                pe.wait_ge(ht_sb, b * (HTS * NC) + (i + 1) * NC)

            def quad(b, T, m, u, first):
                q = T * QUADS + m
                pe.wait_ge(e_dve, q + 1)
                pe.wait_ge(e_act, q + 1)
                if m == 0 and not first:
                    pe.wait_ge(x2_rdy, T - 1)
                s = e_slot(u, m)
                win = a_win[:, QROWS - 2 - 2 * m:2 * QROWS - 2 - 2 * m]
                for c in range(NC):
                    for grp in range(4):
                        last = mm(ps[QROWS * grp:QROWS * (grp + 1), 4 * u + c, :], win,
                                  E[:, s + grp, c * CH:(c + 1) * CH], start=(m == 0), stop=(m == QUADS - 1),
                                  tile_position=(0, QROWS * grp))
                last.then_inc(e_used, 1)

            def probs_t1(T, u):
                pe.wait_ge(p1_rdy, T + 1)
                transposes(lambda t: T1[:, t * P:(t + 1) * P], 4 * u, pt1_ps)

            def out1(T, u):
                pe.wait_ge(pt1_act, T + 1)
                pe.wait_ge(pt1_dve, T + 1)
                for j in range(NT):
                    last = mm(ps[:, 4 * u, 0:D], PT1[:, j * P:(j + 1) * P], H[:, j, :], start=(j == 0), stop=(j == NT - 1))
                last.then_inc(o1_ps, 1)

            def tile1(b, t, u, tail, first):
                T = b * NT + t
                for m in range(QUADS):
                    quad(b, T, m, u, first)
                    if tail and m == 6:
                        probs_t1(T - 1, 1 - u)
                    if tail and m == 9:
                        out1(T - 1, 1 - u)

            def scores2(b, s, t, h, u, first):
                if h == 0:
                    pe.wait_ge(qcur_rdy, b * NT + t + 1)
                if not first:
                    pe.wait_ge(t2_rdy, s)
                for c in range(NC):
                    last = mm(ps[:, c, :], qcur[:, u, h, :], kst[:, h, c * CH:(c + 1) * CH], start=True, stop=True)
                last.then_inc(s2_ps, 1)

            def probs_t2(r, h, g):
                if g == 0:
                    pe.wait_ge(p2_rdy, r + 1)
                for k in range(TPC):
                    j = g * TPC + k
                    last = nc.tensor.transpose(ps[:, 4 + g % 2, k * P:(k + 1) * P], T2[:, h, j * P:(j + 1) * P],
                                               ident[:, :])
                last.then_inc(pt2_ps, 1)

            def values2(r, h, g, first):
                if g == 0 and not first:
                    pe.wait_ge(att_rdy, r - 1)
                if g < NC - 1:
                    pe.wait_ge(pt2_act, r * 3 + g + 1)
                else:
                    pe.wait_ge(pt2_dve, r + 1)
                for k in range(TPC):
                    last = mm(ps[HD * k:HD * (k + 1), 6 + h % 2, 0:P], V[:, g * TPC + k, h * HD:(h + 1) * HD],
                              PT2[:, g, k * P:(k + 1) * P], start=(g == 0), stop=(g == NC - 1),
                              tile_position=(0, HD * k))
                if g == NC - 1:
                    last.then_inc(o2_ps, 1)

            def combine2(r, h):
                pe.wait_ge(o4_rdy, r + 1)
                mm(ps[:, 6 + h % 2, P:P + HD], o4[:, h % 2, :], sel[:, :], start=True, stop=True).then_inc(c2_ps, 1)

            def step2(b, s, t, h, u, loc=None):
                def there(lag):
                    return loc is None or 0 <= loc - lag < STEPS

                h2, h3 = ((h - k) % HEADS for k in (2, 3))
                if there(0):
                    scores2(b, s, t, h, u, loc == 0)
                if there(4):
                    combine2(s - 4, h)
                if there(3):
                    values2(s - 3, h3, 0, loc is not None and loc < 5)
                    values2(s - 3, h3, 1, False)
                if there(2):
                    if there(3):
                        pe.wait_ge(pt2_act, (s - 2) * 3)
                        pe.wait_ge(pt2_dve, s - 2)
                    probs_t2(s - 2, h2, 0)
                    probs_t2(s - 2, h2, 1)
                if there(3):
                    values2(s - 3, h3, 2, False)
                    values2(s - 3, h3, 3, False)
                if there(2):
                    pe.wait_ge(pt2_act, (s - 2) * 3 + 1)
                    probs_t2(s - 2, h2, 2)
                    pe.wait_ge(pt2_act, (s - 2) * 3 + 2)
                    probs_t2(s - 2, h2, 3)

            with pe.Fori(0, NB) as b:
                for l in range(LAYERS):
                    h_transposes(b, l)
                    for t in range(NT):
                        last = mm(ps[:, 4 + t // TPC, (t % TPC) * P:(t % TPC + 1) * P], HT[:, t * P:(t + 1) * P],
                                  w0[:, l, :], start=True, stop=True)
                        if t % TPC == TPC - 1:
                            last.then_inc(hw_ps, 1)
                    pe.wait_ge(hw_sb, b * (LAYERS * NC) + (l + 1) * NC)
                    if l == 0:
                        pe.wait_ge(adj_in, (b + 1) * (16 * NT))
                    for c in range(NC):
                        for t in range(NT):
                            last = mm(ps[:, c, :], HW[:, t * P:(t + 1) * P], A[:, t, c * CH:(c + 1) * CH],
                                      start=(t == 0), stop=(t == NT - 1))
                        last.then_inc(agg_ps, 1)
                    if l == 0:
                        pe.wait_ge(deg_rdy, (b + 1) * NT)
                    pe.wait_ge(agg_sb, b * (LAYERS * NC) + (l + 1) * NC)
                    transposes(lambda t: AGG[:, t * P:(t + 1) * P], 4, z_ps)
                h_transposes(b, LAYERS)
                for c in range(NC):
                    mm(ps[:, 4 + c, :], w1t2[:, :], HT[:, c * CH:(c + 1) * CH], start=True, stop=True).then_inc(qk1_ps, 1)
                pairs = HT[:, :].rearrange("p (g two) -> p g two", two=2)
                for c in range(2):
                    for two in range(2):
                        last = mm(ps[DG * two:DG * (two + 1), c, :], w2t[:, :], pairs[:, c * CH:(c + 1) * CH, two],
                                  start=True, stop=True, tile_position=(0, DG * two))
                    last.then_inc(qk1_ps, 1)
                pe.wait_ge(qk1_sb, (b + 1) * 6)
                tile1(b, 0, 0, False, True)
                tile1(b, 1, 1, True, True)
                with pe.Fori(1, NT // 2) as tt:
                    tile1(b, tt * 2, 0, True, False)
                    tile1(b, tt * 2 + 1, 1, True, False)
                probs_t1(b * NT + NT - 1, 1)
                out1(b * NT + NT - 1, 1)
                h_transposes(b, LAYERS + 1)
                for bank, w in ((4, wq), (0, wk)):
                    for c in range(NC):
                        mm(ps[:, bank + c, :], w[:, :], HT[:, c * CH:(c + 1) * CH], start=True, stop=True).then_inc(qk2_ps, 1)
                pe.wait_ge(qk2_act, b * 8 + 4)
                for t in range(NT):
                    last = mm(ps[:, 4 + t // TPC, (t % TPC) * P:(t % TPC + 1) * P], HT[:, t * P:(t + 1) * P], wv[:, :],
                              start=True, stop=True)
                    if t % TPC == TPC - 1:
                        last.then_inc(v_ps, 1)
                pe.wait_ge(v_sb, (b + 1) * NC)
                pe.wait_ge(qk2_act, (b + 1) * 8)
                pe.wait_ge(st_in, (b + 1) * (16 * 32))
                S0 = b * (NT * HEADS)
                for t in range(2):
                    for h in range(HEADS):
                        step2(b, S0 + t * HEADS + h, t, h, t, t * HEADS + h)
                with pe.Fori(1, NT // 2) as tt:
                    for u in range(2):
                        for h in range(HEADS):
                            step2(b, S0 + tt * (2 * HEADS) + (HEADS * u + h), tt * 2 + u, h, u)
                for loc in range(STEPS, STEPS + 4):
                    step2(b, S0 + loc, NT, loc % HEADS, 0, loc)
                pe.wait_ge(att_rdy, (b + 1) * (NT * HEADS))
                transposes(lambda t: H[:, t, :], 0, at_ps)
                for t in range(NT):
                    if t % TPC == 0:
                        pe.wait_ge(at_sb, b * NC + t // TPC + 1)
                    last = mm(ps[:, 4 + t // TPC, (t % TPC) * P:(t % TPC + 1) * P], HT[:, t * P:(t + 1) * P], wo[:, :],
                              start=True, stop=True)
                    if t % TPC == TPC - 1:
                        last.then_inc(x3_ps, 1)
                with pe.Fori(0, NT // 2) as tt:
                    for u in range(2):
                        T = b * NT + tt * 2 + u
                        if u:
                            pe.wait_ge(at3_act, T * 2)
                        pe.wait_ge(diag_rdy, b * (NT + 1) + tt * 2 + (u + 2))
                        for j in range(NT):
                            g = j // TPC
                            last = nc.tensor.transpose(ps[:, (4 * u + g) % 6, (j % TPC) * P:(j % TPC + 1) * P],
                                                       ring[:, u, j * P:(j + 1) * P], ident[:, :])
                            if j % TPC == TPC - 1:
                                last.then_inc(at3_ps, 1)
                    for u in range(2):
                        T = b * NT + tt * 2 + u
                        AT = (AGG, HT)[u]
                        pe.wait_ge(at3_act, (T + 1) * 2)
                        pe.wait_ge(at3_dve, (T + 1) * 2)
                        pe.wait_ge(o3_rdy, T + 2)
                        for j in range(NT):
                            last = mm(ps[:, 6 + u, 0:P], H[:, j, :], AT[:, j * P:(j + 1) * P],
                                      start=(j == 0), stop=(j == NT - 1))
                            if j == 0:
                                last.then_inc(ring_free, 1)
                        last.then_inc(hb_ps, 1)
                    for u in range(2):
                        T = b * NT + tt * 2 + u
                        pe.wait_ge(hb_sb, T + 1)
                        mm(ps[:, 6 + u, P:2 * P], hbT[:, u, :], wb[:, :], start=True, stop=True).then_inc(o3_ps, 1)


_INS = ["x", "adj", "L0_gnn_Ws", "L0_gnn_bs", "L0_gnn_gammas", "L0_gnn_betas", "L1_gnn_W1", "L1_gnn_W2", "L1_gnn_a",
        "L2_gnn_Wq", "L2_gnn_bq", "L2_gnn_Wk", "L2_gnn_bk", "L2_gnn_Wv", "L2_gnn_bv", "L2_gnn_Wo", "L2_gnn_bo",
        "L3_gnn_B"]


def kernel(**inputs):
    import numpy as np
    import concourse.bacc as bacc
    from concourse.bass_utils import run_bass_kernel_spmd

    nc = bacc.Bacc("TRN2", target_bir_lowering=False, num_devices=1)
    arrays, args = {}, []
    for name in _INS:
        a = np.ascontiguousarray(inputs[name])
        arrays[f"in_{name}"] = a
        args.append(nc.dram_tensor(f"in_{name}", a.shape, mybir.dt.from_np(a.dtype), kind="ExternalInput").ap())
    args.append(nc.dram_tensor("out_x", (NB, N, D), F32, kind="ExternalOutput").ap())
    build(nc, *args)
    r = run_bass_kernel_spmd(nc, [arrays], core_ids=[0])
    return r.results[0]["out_x"]
```

```python
from contextlib import ExitStack

import concourse.bass as bass
from concourse import mybir

F32 = mybir.dt.float32
F32R = mybir.dt.float32r
ALU = mybir.AluOpType
ACT = mybir.ActivationFunctionType

P = 128
NB, N, D = 8, 2048, 128
NT = N // P
CH = 512
NC = N // CH
TPC = NT // NC
LAYERS = 3
HEADS, HD = 4, 32
DG = 64
QUADS = 16
QROWS = P // 4
LN_EPS = 1e-5
BIG = 3.0e38
MASK_ADD = 1e22
MASK_DOT = 1e9
SCALE = float(1.0 / (HD ** 0.5))
LNS = LAYERS + 4
HTS = LAYERS + 2
HEV = LAYERS + 3
HALF = 8
LN_ORDER = [(i, half) for i in range(LAYERS) for half in range(2)]
LN_ORDER += [(LAYERS, 0), (LAYERS + 1, 0), (LAYERS, 1), (LAYERS + 1, 1)]
LN_ORDER += [(i, half) for i in range(LAYERS + 2, LNS) for half in range(2)]
DVE_STEPS = 2 * LNS + 4 * LAYERS + 7
STEPS = NT * HEADS


EQ = 3
TURN = QUADS + QUADS // 2


def e_slot(u, m):
    return 4 * ((u * QUADS + m - TURN) % (2 * QUADS) % EQ)


def e_lag(u, m):
    return 2 if u * QUADS + m - TURN in (0, 1) else EQ


class Steps:

    def __init__(self, sem, per_batch):
        self.sem, self.per_batch, self.k = sem, per_batch, 0

    def done(self, ins):
        self.k += 1
        ins.then_inc(self.sem, 1)

    def wait(self, eng, b):
        eng.wait_ge(self.sem, b * self.per_batch + self.k)


def build(nc, x, adj, Ws, bs, gammas, betas, W1, W2, a_vec, Wq, bq, Wk, bk, Wv, bv, Wo, bo, Bw, out):
    x_v = x.rearrange("b (t p) d -> b p t d", p=P)
    out_v = out.rearrange("b (t p) d -> b p t d", p=P)
    adj_v = adj.rearrange("b (t p) n -> b t p n", p=P)

    with ExitStack() as ctx:
        def sb(name, shape, dt=F32, where=None):
            return (where or ctx).enter_context(nc.sbuf_tensor(name, shape, dt))

        def sem(name):
            return ctx.enter_context(nc.semaphore(name))

        ring = sb("adj_ring", [P, 2, N])
        X = sb("X", [P, NT, D])
        H = sb("H", [P, NT, D])
        HT = sb("HT", [P, N])
        HW = sb("HW", [P, N])
        AGG = sb("AGG", [P, N])
        ident = sb("ident", [P, P])
        w0 = sb("w0", [P, LAYERS, D])
        b0 = sb("b0", [P, LAYERS])
        gam = sb("gam", [P, LAYERS, D])
        bet = sb("bet", [P, LAYERS, D])
        w12 = sb("w12", [P, D])
        w1t2 = sb("w1t2", [P, P])
        w2t = sb("w2t", [P, DG])
        a_col = sb("a_col", [P, 1])
        a_win = sb("a_win", [P, 2 * QROWS - 2])
        wq = sb("wq", [P, D])
        wk = sb("wk", [P, D])
        wv = sb("wv", [P, D])
        wo = sb("wo", [P, D])
        wb = sb("wb", [P, D])
        bq_c = sb("bq_c", [P, 1])
        bqs_c = sb("bqs_c", [P, 1])
        bk_c = sb("bk_c", [P, 1])
        bv_b = sb("bv_b", [P, D])
        bo_b = sb("bo_b", [P, D])
        halves = sb("halves", [P, NT])
        epses = sb("epses", [P, NT])
        ones = sb("ones", [P, NT])
        stats = sb("stats", [P, NT, 6])
        mv = sb("mv", [P, NT, 2])
        var = sb("var", [P, NT])
        rstd = sb("rstd", [P, NT])
        deg = sb("deg", [P, NT])
        deg1 = sb("deg1", [P, NT])
        dinv = sb("dinv", [P, NT])
        kd = sb("kd", [P, 2, 64])
        ka = sb("ka", [P, 2, 64])
        nmin1 = sb("nmin1", [P, 2])
        rsum1 = sb("rsum1", [P, 2])
        rinv1 = sb("rinv1", [P, 2])
        nmin2 = sb("nmin2", [P, HEADS])
        rsum2 = sb("rsum2", [P, HEADS])
        rinv2 = sb("rinv2", [P, HEADS])
        qcur = sb("qcur", [P, 2, HEADS, P], F32R)
        sel = sb("sel", [P, HD])
        o4 = sb("o4", [P, 2, P])
        hbT = sb("hbT", [P, 2, P])

        with ExitStack() as ph:
            A = sb("adj_res", [P, NT, N], where=ph)
        with ExitStack() as ph:
            E = sb("E", [P, 4 * EQ, N], where=ph)
            Q2 = sb("Q2", [P, N], where=ph)
            K2 = sb("K2", [P, N // 2], where=ph)
            T1 = sb("T1", [P, N], where=ph)
            PT1 = sb("PT1", [P, N], where=ph)
        with ExitStack() as ph:
            kst = sb("kst", [P, HEADS, N], F32R, where=ph)
            qst = sb("qst", [P, HEADS, N], F32R, where=ph)
            V = sb("V", [P, NT, D], where=ph)
            PT2 = sb("PT2", [P, NC, CH], where=ph)
            with ExitStack() as sub:
                T2 = sb("T2", [P, HEADS, N], where=sub)
            with ExitStack() as sub:
                qh = sb("qh", [P, N], F32R, where=sub)
                ql = sb("ql", [P, N], F32R, where=sub)
                kh = sb("kh", [P, N], F32R, where=sub)
                kl = sb("kl", [P, N], F32R, where=sub)

        ps = ctx.enter_context(nc.psum_tensor("ps", [P, 8, CH], F32))

        waited = sem("waited")
        mask2_rdy = sem("mask2_rdy")
        const_in = sem("const_in")
        const_w = sem("const_w")
        w12_ps = sem("w12_ps")
        const_rdy = sem("const_rdy")
        id_rdy = sem("id_rdy")
        x_in = sem("x_in")
        adj_in = sem("adj_in")
        ring_in = [sem("ring_in0"), sem("ring_in1")]
        ring_free = sem("ring_free")
        dve_self = sem("dve_self")
        pool_self = sem("pool_self")
        ln_stats = sem("ln_stats")
        ln_rstd = sem("ln_rstd")
        deg_rdy = sem("deg_rdy")
        dinv_rdy = sem("dinv_rdy")
        zn_rdy = sem("zn_rdy")
        h_rdy = sem("h_rdy")
        ht_ps = sem("ht_ps")
        ht_sb = sem("ht_sb")
        hw_ps = sem("hw_ps")
        hw_sb = sem("hw_sb")
        agg_ps = sem("agg_ps")
        agg_sb = sem("agg_sb")
        z_ps = sem("z_ps")
        qk1_ps = sem("qk1_ps")
        qk1_sb = sem("qk1_sb")
        kd_rdy = sem("kd_rdy")
        ka_rdy = sem("ka_rdy")
        e_dve = sem("e_dve")
        e_act = sem("e_act")
        e_used = sem("e_used")
        mask1 = sem("mask1")
        t1_rdy = sem("t1_rdy")
        p1_rdy = sem("p1_rdy")
        pt1_ps = sem("pt1_ps")
        pt1_act = sem("pt1_act")
        pt1_dve = sem("pt1_dve")
        rinv1_rdy = sem("rinv1_rdy")
        o1_ps = sem("o1_ps")
        x2_rdy = sem("x2_rdy")
        qk2_ps = sem("qk2_ps")
        qk2_act = sem("qk2_act")
        qk2_dve = sem("qk2_dve")
        v_ps = sem("v_ps")
        v_sb = sem("v_sb")
        stq_in = sem("stq_in")
        stk_in = [sem(f"stk_in{h}") for h in range(HEADS)]
        qcur_rdy = sem("qcur_rdy")
        s2_ps = sem("s2_ps")
        t2_rdy = sem("t2_rdy")
        p2_rdy = sem("p2_rdy")
        pt2_ps = sem("pt2_ps")
        pt2_act = sem("pt2_act")
        pt2_dve = sem("pt2_dve")
        rinv2_rdy = sem("rinv2_rdy")
        o2_ps = sem("o2_ps")
        o4_rdy = sem("o4_rdy")
        c2_ps = sem("c2_ps")
        att_rdy = sem("att_rdy")
        at_ps = sem("at_ps")
        at_sb = sem("at_sb")
        x3_ps = sem("x3_ps")
        g_norm = sem("g_norm")
        g_rdy = sem("g_rdy")
        diag_rdy = sem("diag_rdy")
        at3_ps = sem("at3_ps")
        at3_act = sem("at3_act")
        at3_dve = sem("at3_dve")
        hb_ps = sem("hb_ps")
        hb_sb = sem("hb_sb")
        o3_ps = sem("o3_ps")
        o3_rdy = sem("o3_rdy")
        cleared = sem("cleared")
        out_done = sem("out_done")

        CONST_DMAS = 16
        block = ctx.enter_context(nc.Block())

        def alone(eng):
            eng.sem_inc(waited, 1)

        def tcols(t):
            return bass.ds(t * P, P)

        @block.sync
        def _(sp):
            def const(dst, src):
                sp.dma_start(dst, src).then_inc(const_in, 16)

            def bcast(src, n):
                return src.rearrange("(o e) -> o e", o=1).broadcast_to([P, n])

            const(w0[:, :, :], Ws.rearrange("l d e -> d l e"))
            with nc.allow_non_contiguous_dma(reason="one small load"):
                const(b0[:, :], bs.rearrange("l e -> e l"))
            const(gam[:, :, :].rearrange("p l e -> p (l e)"), bcast(gammas.rearrange("l e -> (l e)"), LAYERS * D))
            const(bet[:, :, :].rearrange("p l e -> p (l e)"), bcast(betas.rearrange("l e -> (l e)"), LAYERS * D))
            const(w12[0:DG, :], W1)
            const(w12[DG:P, :], W2)
            const(a_col[0:DG, :], a_vec.rearrange("(e o) -> e o", o=1))
            const(a_col[DG:P, :], a_vec.rearrange("(e o) -> e o", o=1))
            for dst, src in ((wq, Wq), (wk, Wk), (wv, Wv), (wo, Wo), (wb, Bw)):
                const(dst[:, :], src)
            const(bq_c[:, :], bq.rearrange("(e o) -> e o", o=1))
            const(bk_c[:, :], bk.rearrange("(e o) -> e o", o=1))
            const(bo_b[:, :], bcast(bo, D))
            sp.dma_start(bv_b[:, :], bcast(bv, D)).then_inc(out_done, 16)
            with sp.Fori(0, NB) as b:
                for t in range(NT):
                    sp.wait_ge(o3_rdy, b * NT + t + 4)
                    sp.dma_start(X[:, t, :], x_v[bass.ds(b, 1), :, t].rearrange("o p d -> p (o d)")).then_inc(x_in, 16)
                for phase in range(3):
                    with sp.Fori(0, NT // 2) as tt:
                        for u in range(2):
                            sp.wait_ge(ring_free, b * (3 * NT) + tt * 2 + (phase * NT + u + 1))
                            sp.dma_start(ring[:, u, :],
                                         adj_v[bass.ds(b, 1), bass.ds(tt * 2 + u, 1)].rearrange("o c p n -> p (o c n)")
                                         ).then_inc(ring_in[u], 16)
                sp.wait_ge(o3_rdy, b * NT + (2 * NT + 3))
                sp.dma_start(out_v[bass.ds(b, 1)].rearrange("o p t d -> p (o t) d"),
                             HW[:, :].rearrange("p (t d) -> p t d", t=NT)).then_inc(out_done, 16)
            sp.wait_ge(out_done, 16 * (NB + 1))

        def ring_wait(eng, b, phase, half, u):
            eng.wait_ge(ring_in[u], b * (16 * 24) + half * 16 + 16 * (phase * 8 + 1))

        @block.gpsimd
        def _(pool):
            pool.memset(ident[:, :], 0.0).then_inc(pool_self, 1)
            pool.memset(halves[:, :], -0.5).then_inc(pool_self, 1)
            pool.memset(epses[:, :], LN_EPS).then_inc(pool_self, 1)
            pool.memset(ones[:, :], 1.0).then_inc(pool_self, 1)
            pool.wait_ge(pool_self, 4)
            pool.affine_select(out=ident[:, :], in_=ident[:, :], compare_op=ALU.not_equal, fill=1.0, base=0,
                               pattern=[[-1, P]], channel_multiplier=1).then_inc(id_rdy, 1)
            own = Steps(pool_self, 2 * LNS + 1)
            own.k = 4

            def rstd_step(b, k):
                half = LN_ORDER[k][1]
                t = slice(half * HALF, (half + 1) * HALF)
                pool.wait_ge(ln_stats, b * (2 * LNS) + k + 1)
                own.done(pool.tensor_tensor(var[:, t], mv[:, t, 1], epses[:, t], ALU.add))
                own.wait(pool, b)
                pool.tensor_tensor(rstd[:, t], var[:, t], halves[:, t], ALU.pow).then_inc(ln_rstd, 1)

            with pool.Fori(0, NB) as b:
                own.k = 4
                for t in range(NT):
                    pool.wait_ge(hb_sb, b * NT + t + 1)
                    pool.dma_start(A[:, t, :], adj_v[bass.ds(b, 1), t].rearrange("o p n -> p (o n)")).then_inc(adj_in, 16)
                for k in range(2 * (LAYERS + 2)):
                    rstd_step(b, k)
                pool.wait_ge(deg_rdy, (b + 1) * NT)
                own.done(pool.tensor_tensor(deg1[:, :], deg[:, :], ones[:, :], ALU.add))
                own.wait(pool, b)
                pool.tensor_tensor(dinv[:, :], deg1[:, :], halves[:, :], ALU.pow).then_inc(dinv_rdy, 1)
                for k in range(2 * (LAYERS + 2), 2 * LNS):
                    rstd_step(b, k)

        @block.scalar
        def _(act):
            def evac(dst, src):
                return nc.scalar.activation(dst, src, ACT.Copy)

            def relu(b, e, src, g):
                act.wait_ge(zn_rdy, (b * HEV + e) * NC + g + 1)
                nc.scalar.activation(H[:, g * TPC:(g + 1) * TPC, :].rearrange("p t d -> p (t d)"),
                                     src[:, g * CH:(g + 1) * CH], ACT.Relu).then_inc(h_rdy, 1)

            def evac_ht(b, i, c):
                act.wait_ge(ht_ps, b * (HTS * NC) + i * NC + c + 1)
                evac(HT[:, c * CH:(c + 1) * CH], ps[:, c, :]).then_inc(ht_sb, 1)

            def h_section(b, i, e, src, after, mid=None):
                relu(b, e, src, 0)
                relu(b, e, src, 1)
                if mid:
                    mid()
                evac_ht(b, i, 0)
                evac_ht(b, i, 1)
                after(0)
                after(1)
                relu(b, e, src, 2)
                evac_ht(b, i, 2)
                relu(b, e, src, 3)
                after(2)
                evac_ht(b, i, 3)
                after(3)

            def evac_hw(b, l, g):
                if l == 0 and g == 0:
                    act.wait_ge(out_done, b * 16 + 16)
                act.wait_ge(hw_ps, b * (LAYERS * NC) + l * NC + g + 1)
                evac(HW[:, g * CH:(g + 1) * CH], ps[:, 4 + g, :]).then_inc(hw_sb, 1)

            def evac_agg(b, l, c):
                act.wait_ge(agg_ps, b * (LAYERS * NC) + l * NC + c + 1)
                nc.scalar.activation(AGG[:, c * CH:(c + 1) * CH], ps[:, c, :], ACT.Identity,
                                     bias=b0[:, l:l + 1]).then_inc(agg_sb, 1)

            def evac_q1(b, c):
                act.wait_ge(qk1_ps, b * 6 + c + 1)
                evac(Q2[:, c * CH:(c + 1) * CH], ps[:, 4 + c, :]).then_inc(qk1_sb, 1)

            def evac_q2(b, c):
                act.wait_ge(qk2_ps, b * 8 + c + 1)
                nc.scalar.activation(HW[:, c * CH:(c + 1) * CH], ps[:, 4 + c, :], ACT.Identity,
                                     bias=bqs_c[:, 0:1], scale=-SCALE).then_inc(qk2_act, 1)

            def degrees(b, t, T, half, u, tail):
                if tail:
                    act.wait_ge(o1_ps, T)
                ring_wait(act, b, 0, half, u)
                nc.scalar.activation(PT1[:, :], ring[:, u, :], ACT.Copy,
                                     accum_out=deg[:, bass.ds(t, 1)]).then_inc(deg_rdy, 1)

            def keys(t, T, u, first):
                if not first:
                    act.wait_ge(e_act, (T - 1) * QUADS)
                evac(ka[:, u, :], K2[:, bass.ds(t * 64, 64)]).then_inc(ka_rdy, 1)
                act.wait_ge(ka_rdy, T + 1)

            def quad(T, m, u, first):
                if not (first and m < EQ):
                    act.wait_ge(e_used, T * QUADS + (m - e_lag(u, m) + 1))
                s = e_slot(u, m)
                nc.scalar.activation(E[:, s + 2, N // 2:N], Q2[:, N // 2:N], ACT.Relu, bias=ka[:, u, 32 + m:33 + m])
                nc.scalar.activation(E[:, s + 3, :], Q2[:, :], ACT.Relu, bias=ka[:, u, 48 + m:49 + m]).then_inc(e_act, 1)

            def exp1(T, u):
                act.wait_ge(t1_rdy, T + 1)
                nc.scalar.activation(T1[:, :], T1[:, :], ACT.Exp, bias=nmin1[:, u:u + 1], scale=-1.0,
                                     accum_out=rsum1[:, u:u + 1]).then_inc(p1_rdy, 1)

            def evac1(T, u):
                act.wait_ge(deg_rdy, T + 1)
                for g in range(2):
                    act.wait_ge(pt1_ps, T * NC + g + 1)
                    last = evac(PT1[:, g * CH:(g + 1) * CH], ps[:, 4 * u + g, :])
                last.then_inc(pt1_act, 1)

            def tile1(b, t, u, tail, half, first):
                T = b * NT + t
                keys(t, T, u, first)
                for m in range(QUADS):
                    quad(T, m, u, not tail)
                    if tail and m == 4:
                        exp1(T - 1, 1 - u)
                    if tail and m == 7:
                        evac1(T - 1, 1 - u)
                    if m == 12:
                        degrees(b, t, T, half, u, tail)

            def exp2(s, h):
                act.wait_ge(t2_rdy, s + 1)
                nc.scalar.activation(T2[:, h, :], T2[:, h, :], ACT.Exp, bias=nmin2[:, h:h + 1], scale=-1.0,
                                     accum_out=rsum2[:, h:h + 1]).then_inc(p2_rdy, 1)

            def norm2(t, r, h):
                act.wait_ge(rinv2_rdy, r + 1)
                act.wait_ge(c2_ps, r + 1)
                dst = H[:, bass.ds(t, 1), h * HD:(h + 1) * HD].rearrange("p o d -> p (o d)")
                nc.scalar.activation(dst, ps[:, 6 + h % 2, P:P + HD], ACT.Copy, scale=rinv2[:, h:h + 1]
                                     ).then_inc(att_rdy, 1)

            def evac2(r):
                for g in range(3):
                    act.wait_ge(pt2_ps, r * NC + g + 1)
                    evac(PT2[:, g, :], ps[:, 4 + g % 2, :]).then_inc(pt2_act, 1)

            def step2(s, t, h, loc=None):
                def there(lag):
                    return loc is None or 0 <= loc - lag < STEPS

                if there(1):
                    exp2(s - 1, (h - 1) % HEADS)
                if there(4):
                    norm2(t - 1, s - 4, h)
                if there(2):
                    evac2(s - 2)

            act.wait_ge(const_rdy, 1)
            act.sem_inc(hb_sb, NT)
            with act.Fori(0, NB) as b:
                Hf = H[:, :, :].rearrange("p t d -> p (t d)")
                h_section(b, 0, 0, Hf, lambda g: evac_hw(b, 0, g))
                for l in range(LAYERS):
                    for c in range(NC - 1):
                        evac_agg(b, l, c)
                    if l < LAYERS - 1:
                        h_section(b, l + 1, l + 1, HT, lambda g: evac_hw(b, l + 1, g), lambda: evac_agg(b, l, NC - 1))
                    else:
                        for g in range(NC):
                            if g == 2:
                                evac_agg(b, l, NC - 1)
                            relu(b, LAYERS, HT, g)
                h_section(b, LAYERS, LAYERS + 1, Hf, lambda c: evac_q1(b, c))
                for c in range(2):
                    act.wait_ge(qk1_ps, b * 6 + 4 + c + 1)
                    evac(K2[:, c * CH:(c + 1) * CH], ps[:, c, :]).then_inc(qk1_sb, 1)
                act.wait_ge(qk1_sb, (b + 1) * 6)
                tile1(b, 0, 0, False, 0, True)
                tile1(b, 1, 1, True, 0, True)
                with act.Fori(1, NT // 2) as tt:
                    tile1(b, tt * 2, 0, True, tt, False)
                    tile1(b, tt * 2 + 1, 1, True, tt, False)
                exp1(b * NT + NT - 1, 1)
                evac1(b * NT + NT - 1, 1)
                h_section(b, LAYERS + 1, LAYERS + 2, Hf, lambda c: evac_q2(b, c))
                for c in range(NC):
                    act.wait_ge(qk2_ps, b * 8 + 4 + c + 1)
                    nc.scalar.activation(AGG[:, c * CH:(c + 1) * CH], ps[:, c, :], ACT.Identity,
                                         bias=bk_c[:, 0:1]).then_inc(qk2_act, 1)
                for dst, parts, k in ((qst, (qh, qh, ql, ql), 1), (kst, (kh, kl, kh, kl), 2)):
                    act.wait_ge(qk2_dve, b * 2 + k)
                    for h in range(HEADS):
                        for blk in range(4):
                            act.dma_start(dst[HD * blk:HD * (blk + 1), h, :].bitcast(F32),
                                          parts[blk][HD * h:HD * (h + 1), :].bitcast(F32)
                                          ).then_inc(stq_in if k == 1 else stk_in[h], 16)
                S0 = b * (NT * HEADS)
                for loc in range(HEADS):
                    step2(S0 + loc, 0, loc, loc)
                with act.Fori(1, NT) as t:
                    for h in range(HEADS):
                        step2(S0 + t * HEADS + h, t, h)
                for loc in range(STEPS, STEPS + 4):
                    step2(S0 + loc, NT, loc % HEADS, loc)
                for c in range(NC):
                    act.wait_ge(at_ps, b * NC + c + 1)
                    evac(HT[:, c * CH:(c + 1) * CH], ps[:, c, :]).then_inc(at_sb, 1)
                with act.Fori(0, NT // 2) as tt:
                    for u in range(2):
                        T = b * NT + tt * 2 + u
                        AT = (AGG, HT)[u]
                        for g in range(2):
                            act.wait_ge(at3_ps, T * NC + g + 1)
                            evac(AT[:, g * CH:(g + 1) * CH], ps[:, (4 * u + g) % 6, :]).then_inc(at3_act, 1)
                    for u in range(2):
                        T = b * NT + tt * 2 + u
                        act.wait_ge(hb_ps, T + 1)
                        evac(hbT[:, u, :], ps[:, 6 + u, 0:P]).then_inc(hb_sb, 1)

        @block.vector
        def _(dve):
            own = Steps(dve_self, DVE_STEPS)

            def link(b, ins):
                own.done(ins)
                own.wait(dve, b)

            nc.vector.memset(a_win[:, :], 0.0).then_inc(ring_free, 1)
            nc.vector.memset(mv[:, :, :], 0.0).then_inc(ring_free, 1)
            for buf in (stats[:, :, :], dinv[:, :], rstd[:, :]):
                nc.vector.memset(buf, 0.0).then_inc(cleared, 1)
            dve.wait_ge(ring_free, 2)
            dve.wait_ge(cleared, 3)
            dve.sem_inc(o3_rdy, NT + 3)
            dve.wait_ge(out_done, 16)
            dve.wait_ge(const_in, 16 * CONST_DMAS)
            nc.vector.tensor_scalar(a_win[0:DG, QROWS - 2:QROWS - 1], a_col[0:DG, :], -1.0, None, ALU.mult)
            nc.vector.tensor_scalar(a_win[DG:P, QROWS - 1:QROWS], a_col[DG:P, :], -1.0, None, ALU.mult)
            nc.vector.tensor_scalar(bqs_c[:, :], bq_c[:, :], -SCALE, None, ALU.mult)
            dve.wait_ge(id_rdy, 1)
            for k in range(P // HD):
                nc.vector.tensor_copy(sel[HD * k:HD * (k + 1), :], ident[HD * k:HD * (k + 1), HD * k:HD * (k + 1)])
            dve.wait_ge(w12_ps, 1)
            nc.vector.tensor_copy(w1t2[:, 0:DG], ps[:, 0, 0:DG])
            nc.vector.tensor_copy(w1t2[:, DG:P], ps[:, 0, 0:DG])
            nc.vector.tensor_copy(w2t[:, :], ps[:, 0, DG:P]).then_inc(const_rdy, 1)

            def tiles_of(half):
                return range(half * HALF, (half + 1) * HALF)

            def norm_stats(b, half, src):
                for t in tiles_of(half):
                    last = nc.vector.bn_stats(stats[:, t, :], src[:, t, :])
                link(b, last)
                alone(dve)
                for t in tiles_of(half):
                    last = nc.vector.bn_aggr(mv[:, t, :], stats[:, t, :])
                last.then_inc(ln_stats, 1)

            def normalise(b, i, half, src, dst, done):
                dve.wait_ge(ln_rstd, b * (2 * LNS) + LN_ORDER.index((i, half)) + 1)
                for t in tiles_of(half):
                    last = nc.vector.tensor_scalar(dst[:, t, :], src[:, t, :], mv[:, t, 0:1], rstd[:, t:t + 1],
                                                   ALU.subtract, ALU.mult)
                    if t % TPC == TPC - 1:
                        last.then_inc(done, 1)

            def normalise_affine(b, i, half, Z, l):
                for t in tiles_of(half):
                    last = nc.vector.scalar_tensor_tensor(out=Z[:, t, :], in0=Z[:, t, :], scalar=mv[:, t, 0:1],
                                                          in1=gam[:, l, :], op0=ALU.subtract, op1=ALU.mult)
                link(b, last)
                dve.wait_ge(ln_rstd, b * (2 * LNS) + LN_ORDER.index((i, half)) + 1)
                for t in tiles_of(half):
                    last = nc.vector.scalar_tensor_tensor(out=Z[:, t, :], in0=Z[:, t, :], scalar=rstd[:, t:t + 1],
                                                          in1=bet[:, l, :], op0=ALU.mult, op1=ALU.add)
                    if t % TPC == TPC - 1:
                        last.then_inc(zn_rdy, 1)

            def residual(b, half):
                for g in (2 * half, 2 * half + 1):
                    dve.wait_ge(h_rdy, (b * HEV + LAYERS) * NC + g + 1)
                    xg = X[:, g * TPC:(g + 1) * TPC, :]
                    last = nc.vector.tensor_tensor(xg, xg, H[:, g * TPC:(g + 1) * TPC, :], ALU.add)
                link(b, last)
                norm_stats(b, half, X)

            def tiles(buf):
                return buf[:, :].rearrange("p (t d) -> p t d", t=NT)

            def over_tiles(row):
                return row.rearrange("p (o d) -> p o d", o=1).broadcast_to([P, NT, D])

            def keys(t, T, u, first):
                if not first:
                    dve.wait_ge(e_dve, (T - 1) * QUADS)
                nc.vector.tensor_copy(kd[:, u, :], K2[:, bass.ds(t * 64, 64)]).then_inc(kd_rdy, 1)
                dve.wait_ge(kd_rdy, T + 1)

            def quad(T, m, u, first):
                if not (first and m < EQ):
                    dve.wait_ge(e_used, T * QUADS + (m - e_lag(u, m) + 1))
                s = e_slot(u, m)
                nc.vector.tensor_scalar(E[:, s, :], Q2[:, :], kd[:, u, m:m + 1], 0.0, ALU.add, ALU.max)
                nc.vector.tensor_scalar(E[:, s + 1, :], Q2[:, :], kd[:, u, 16 + m:17 + m], 0.0, ALU.add, ALU.max)
                nc.vector.tensor_scalar(E[:, s + 2, 0:N // 2], Q2[:, 0:N // 2], kd[:, u, 32 + m:33 + m], 0.0,
                                        ALU.add, ALU.max).then_inc(e_dve, 1)

            def mask1_tile(b, T, half, u):
                ring_wait(dve, b, 0, half, u)
                dve.wait_ge(deg_rdy, T + 1)
                nc.vector.tensor_scalar(ring[:, u, :], ring[:, u, :], 0.0, MASK_ADD, ALU.is_le, ALU.mult
                                        ).then_inc(mask1, 1)

            def min1(T, u):
                dve.wait_ge(e_used, (T + 1) * QUADS)
                dve.wait_ge(mask1, T + 1)
                alone(dve)
                nc.vector.tensor_tensor_reduce(
                    out=T1[:, :], in0=ps[:, 4 * u:4 * u + 4, :].rearrange("p c n -> p (c n)"), in1=ring[:, u, :],
                    scale=1.0, scalar=BIG, op0=ALU.add, op1=ALU.min, accum_out=nmin1[:, u:u + 1]
                ).then_inc(t1_rdy, 1)
                dve.wait_ge(t1_rdy, T + 1)
                dve.sem_inc(ring_free, 1)

            def evac1(T, u):
                for g in range(2, 4):
                    dve.wait_ge(pt1_ps, T * NC + g + 1)
                    last = nc.vector.tensor_copy(PT1[:, g * CH:(g + 1) * CH], ps[:, 4 * u + g, :])
                last.then_inc(pt1_dve, 1)

            def finish1(t, T, u):
                dve.wait_ge(p1_rdy, T + 1)
                nc.vector.reciprocal(rinv1[:, u:u + 1], rsum1[:, u:u + 1]).then_inc(rinv1_rdy, 1)
                dve.wait_ge(rinv1_rdy, T + 1)
                dve.wait_ge(o1_ps, T + 1)
                xt = X[:, bass.ds(t, 1), :].rearrange("p o d -> p (o d)")
                nc.vector.scalar_tensor_tensor(out=xt, in0=ps[:, 4 * u, 0:D], scalar=rinv1[:, u:u + 1], in1=xt,
                                               op0=ALU.mult, op1=ALU.add).then_inc(x2_rdy, 1)

            def tile1(b, t, u, tail, half, first):
                T = b * NT + t
                keys(t, T, u, first)
                for m in range(QUADS):
                    quad(T, m, u, not tail)
                    if tail and m == 2:
                        min1(T - 1, 1 - u)
                    if tail and m == 7:
                        evac1(T - 1, 1 - u)
                    if tail and m == 11:
                        finish1(t - 1, T - 1, 1 - u)
                    if m == 14:
                        mask1_tile(b, T, half, u)

            def queries2(b, t, u):
                nc.vector.tensor_copy(qcur[:, u, :, :], qst[:, :, tcols(t)].bitcast(F32)).then_inc(qcur_rdy, 1)

            def mask2(b, t, half, u):
                ring_wait(dve, b, 1, half, u)
                nc.vector.tensor_scalar(ring[:, u, :], ring[:, u, :], 1.0, -MASK_DOT, ALU.subtract, ALU.mult
                                        ).then_inc(mask2_rdy, 1)

            def min2(s, h, u):
                dve.wait_ge(s2_ps, s + 1)
                alone(dve)
                nc.vector.tensor_tensor_reduce(
                    out=T2[:, h, :], in0=ps[:, 0:4, :].rearrange("p c n -> p (c n)"), in1=ring[:, u, :],
                    scale=1.0, scalar=BIG, op0=ALU.add, op1=ALU.min, accum_out=nmin2[:, h:h + 1]
                ).then_inc(t2_rdy, 1)

            def evac2(r):
                dve.wait_ge(pt2_ps, (r + 1) * NC)
                nc.vector.tensor_copy(PT2[:, NC - 1, :], ps[:, 4 + (NC - 1) % 2, :]).then_inc(pt2_dve, 1)

            def partial2(r, h):
                dve.wait_ge(p2_rdy, r + 1)
                nc.vector.reciprocal(rinv2[:, h:h + 1], rsum2[:, h:h + 1]).then_inc(rinv2_rdy, 1)
                dve.wait_ge(o2_ps, r + 1)
                nc.vector.tensor_copy(o4[:, h % 2, :], ps[:, 6 + h % 2, 0:P]).then_inc(o4_rdy, 1)

            def self_loops(b, tt, u):
                ring_wait(dve, b, 2, tt, u)
                blk = ring[:, u, tcols(tt * 2 + u)]
                nc.vector.tensor_tensor(blk, blk, ident[:, :], ALU.add).then_inc(diag_rdy, 1)

            def pair3(b, tt, more):
                for u in range(2):
                    T = b * NT + tt * 2 + u
                    AT = (AGG, HT)[u]
                    for g in range(2, 4):
                        dve.wait_ge(at3_ps, T * NC + g + 1)
                        nc.vector.tensor_copy(AT[:, g * CH:(g + 1) * CH], ps[:, (4 * u + g) % 6, :]
                                              ).then_inc(at3_dve, 1)
                OUT = tiles(HW)
                for u in range(2):
                    T = b * NT + tt * 2 + u
                    if more:
                        self_loops(b, tt + 1, u)
                    dve.wait_ge(o3_ps, T + 1)
                    t1 = bass.ds(tt * 2 + u, 1)
                    nc.vector.scalar_tensor_tensor(
                        out=OUT[:, t1, :].rearrange("p o d -> p (o d)"), in0=ps[:, 6 + u, P:2 * P],
                        scalar=dinv[:, t1], in1=X[:, t1, :].rearrange("p o d -> p (o d)"),
                        op0=ALU.mult, op1=ALU.add).then_inc(o3_rdy, 1)

            def step2(b, s, t, h, u, loc=None, last=False, half=0):
                def there(lag):
                    return loc is None or 0 <= loc - lag < STEPS

                if there(4):
                    partial2(s - 4, h)
                if there(3):
                    evac2(s - 3)
                if there(0):
                    if h == 0:
                        dve.wait_ge(mask2_rdy, b * NT + t + 1)
                    min2(s, h, u)
                    if h == 1 and not last:
                        queries2(b, t + 1, 1 - u)
                    if h == 2 and not last:
                        mask2(b, t + 1, half, 1 - u)
                    if h == 3:
                        dve.wait_ge(t2_rdy, s + 1)
                        dve.sem_inc(ring_free, 1)

            own.k = 0
            with dve.Fori(0, NB) as b:
                dve.wait_ge(x_in, (b + 1) * (16 * NT))
                for half in range(2):
                    norm_stats(b, half, X)
                for half in range(2):
                    normalise(b, 0, half, X, H, zn_rdy)
                Z = tiles(HT)
                for l in range(LAYERS):
                    for half in range(2):
                        for g in (2 * half, 2 * half + 1):
                            dve.wait_ge(z_ps, b * (LAYERS * NC) + l * NC + g + 1)
                            last = nc.vector.tensor_tensor(
                                Z[:, g * TPC:(g + 1) * TPC, :],
                                ps[:, 4 + g, :].rearrange("p (t d) -> p t d", d=D),
                                H[:, g * TPC:(g + 1) * TPC, :], ALU.add)
                        link(b, last)
                        norm_stats(b, half, Z)
                        dve.wait_ge(ln_stats, b * (2 * LNS) + LN_ORDER.index((l + 1, half)) + 1)
                        normalise_affine(b, l + 1, half, Z, l)
                        if l == LAYERS - 1 and half == 0:
                            residual(b, 0)
                normalise(b, LAYERS + 1, 0, X, H, zn_rdy)
                residual(b, 1)
                normalise(b, LAYERS + 1, 1, X, H, zn_rdy)
                dve.wait_ge(qk1_sb, (b + 1) * 6)
                tile1(b, 0, 0, False, 0, True)
                tile1(b, 1, 1, True, 0, True)
                with dve.Fori(1, NT // 2) as tt:
                    tile1(b, tt * 2, 0, True, tt, False)
                    tile1(b, tt * 2 + 1, 1, True, tt, False)
                T = b * NT + NT - 1
                min1(T, 1)
                evac1(T, 1)
                finish1(NT - 1, T, 1)
                dve.wait_ge(x2_rdy, T + 1)
                for half in range(2):
                    norm_stats(b, half, X)
                for half in range(2):
                    normalise(b, LAYERS + 2, half, X, H, zn_rdy)
                dve.wait_ge(zn_rdy, (b + 1) * (HEV * NC))
                nc.vector.tensor_tensor(X[:, :, :], X[:, :, :], over_tiles(bo_b[:, :]), ALU.add)
                for src, hi, lo, k in ((HW, qh, ql, 0), (AGG, kh, kl, 1)):
                    dve.wait_ge(qk2_act, b * 8 + 4 * (k + 1))
                    link(b, nc.vector.tensor_copy(hi[:, :], src[:, :]))
                    nc.vector.tensor_tensor(lo[:, :], src[:, :], hi[:, :].bitcast(F32), ALU.subtract
                                            ).then_inc(qk2_dve, 1)
                for g in range(NC):
                    dve.wait_ge(v_ps, b * NC + g + 1)
                    nc.vector.tensor_tensor(
                        V[:, g * TPC:(g + 1) * TPC, :], ps[:, 4 + g, :].rearrange("p (t d) -> p t d", d=D),
                        bv_b[:, :].rearrange("p (o d) -> p o d", o=1).broadcast_to([P, TPC, D]), ALU.add
                    ).then_inc(v_sb, 1)
                dve.wait_ge(stq_in, (b + 1) * (16 * 16))
                S0 = b * (NT * HEADS)
                queries2(b, 0, 0)
                mask2(b, 0, 0, 0)
                for loc in range(HEADS):
                    if loc == 2:
                        for h in range(HEADS):
                            dve.wait_ge(stk_in[h], (b + 1) * (16 * 4))
                    step2(b, S0 + loc, 0, loc, 0, loc)
                for h in range(HEADS):
                    step2(b, S0 + HEADS + h, 1, h, 1, half=1)
                with dve.Fori(1, NT // 2 - 1) as tt:
                    for u in range(2):
                        for h in range(HEADS):
                            step2(b, S0 + tt * (2 * HEADS) + (HEADS * u + h), tt * 2 + u, h, u, half=tt + u)
                for t in (NT - 2, NT - 1):
                    for h in range(HEADS):
                        step2(b, S0 + t * HEADS + h, t, h, t % 2, last=(t == NT - 1), half=NT // 2 - 1)
                for loc in range(STEPS, STEPS + 4):
                    step2(b, S0 + loc, NT, loc % HEADS, 0, loc)
                for half in range(2):
                    for g in (2 * half, 2 * half + 1):
                        dve.wait_ge(x3_ps, b * NC + g + 1)
                        xg = X[:, g * TPC:(g + 1) * TPC, :]
                        last = nc.vector.tensor_tensor(xg, ps[:, 4 + g, :].rearrange("p (t d) -> p t d", d=D), xg,
                                                       ALU.add)
                    link(b, last)
                    norm_stats(b, half, X)
                for u in range(2):
                    self_loops(b, 0, u)
                for half in range(2):
                    normalise(b, LAYERS + 3, half, X, H, g_norm)
                dve.wait_ge(g_norm, (b + 1) * NC)
                link(b, nc.vector.tensor_scalar(H[:, :, :], H[:, :, :], 0.0, None, ALU.max))
                dve.wait_ge(dinv_rdy, b + 1)
                nc.vector.tensor_tensor(H[:, :, :], H[:, :, :],
                                        dinv[:, :].rearrange("p (t o) -> p t o", o=1).broadcast_to([P, NT, D]),
                                        ALU.mult).then_inc(g_rdy, 1)
                with dve.Fori(0, NT // 2 - 1) as tt:
                    pair3(b, tt, True)
                pair3(b, NT // 2 - 1, False)
            assert own.k == own.per_batch, own.k

        @block.tensor
        def _(pe):
            mm = nc.tensor.matmul
            pe.wait_ge(const_in, 16 * CONST_DMAS)
            pe.wait_ge(id_rdy, 1)
            nc.tensor.transpose(ps[:, 0, 0:P], w12[:, :], ident[:, :]).then_inc(w12_ps, 1)
            pe.wait_ge(const_rdy, 1)

            def transposes(src, bank, done):
                for t in range(NT):
                    last = nc.tensor.transpose(ps[:, bank + t // TPC, (t % TPC) * P:(t % TPC + 1) * P], src(t), ident[:, :])
                    if t % TPC == TPC - 1:
                        last.then_inc(done, 1)

            def four_transposes(src, g, bank, done):
                for k in range(TPC):
                    last = nc.tensor.transpose(ps[:, bank, k * P:(k + 1) * P], src(g * TPC + k), ident[:, :])
                last.then_inc(done, 1)

            def h_section(b, i, e, work, mid=None):
                def chunk(g):
                    pe.wait_ge(h_rdy, (b * HEV + e) * NC + g + 1)
                    four_transposes(lambda t: H[:, t, :], g, g, ht_ps)

                def product(g):
                    pe.wait_ge(ht_sb, b * (HTS * NC) + i * NC + g + 1)
                    work(g)

                chunk(0)
                chunk(1)
                if mid:
                    mid()
                product(0)
                product(1)
                for g in (2, 3):
                    chunk(g)
                    product(g)

            def project(b, l, g):
                for t in range(g * TPC, (g + 1) * TPC):
                    last = mm(ps[:, 4 + g, (t % TPC) * P:(t % TPC + 1) * P], HT[:, t * P:(t + 1) * P], w0[:, l, :],
                              start=True, stop=True)
                last.then_inc(hw_ps, 1)

            def z_transposes(b, l, c):
                pe.wait_ge(agg_sb, b * (LAYERS * NC) + l * NC + c + 1)
                four_transposes(lambda t: AGG[:, t * P:(t + 1) * P], c, 4 + c, z_ps)

            def quad(b, T, m, u, first):
                q = T * QUADS + m
                pe.wait_ge(e_dve, q + 1)
                pe.wait_ge(e_act, q + 1)
                if m == 0 and not first:
                    pe.wait_ge(x2_rdy, T - 1)
                s = e_slot(u, m)
                win = a_win[:, QROWS - 2 - 2 * m:2 * QROWS - 2 - 2 * m]
                for c in range(NC):
                    for grp in range(4):
                        last = mm(ps[QROWS * grp:QROWS * (grp + 1), 4 * u + c, :], win,
                                  E[:, s + grp, c * CH:(c + 1) * CH], start=(m == 0), stop=(m == QUADS - 1),
                                  tile_position=(0, QROWS * grp))
                last.then_inc(e_used, 1)

            def probs_t1(T, u):
                pe.wait_ge(p1_rdy, T + 1)
                transposes(lambda t: T1[:, t * P:(t + 1) * P], 4 * u, pt1_ps)

            def out1(T, u):
                pe.wait_ge(pt1_act, T + 1)
                pe.wait_ge(pt1_dve, T + 1)
                for j in range(NT):
                    last = mm(ps[:, 4 * u, 0:D], PT1[:, j * P:(j + 1) * P], H[:, j, :], start=(j == 0), stop=(j == NT - 1))
                last.then_inc(o1_ps, 1)

            def tile1(b, t, u, tail, first):
                T = b * NT + t
                for m in range(QUADS):
                    quad(b, T, m, u, first)
                    if tail and m == 6:
                        probs_t1(T - 1, 1 - u)
                    if tail and m == 9:
                        out1(T - 1, 1 - u)

            def scores2(b, s, t, h, u, first, early):
                if h == 0:
                    pe.wait_ge(qcur_rdy, b * NT + t + 1)
                if early:
                    pe.wait_ge(stk_in[h], (b + 1) * (16 * 4))
                if not first:
                    pe.wait_ge(t2_rdy, s)
                for c in range(NC):
                    last = mm(ps[:, c, :], qcur[:, u, h, :], kst[:, h, c * CH:(c + 1) * CH], start=True, stop=True)
                last.then_inc(s2_ps, 1)

            def probs_t2(r, h, g):
                if g == 0:
                    pe.wait_ge(p2_rdy, r + 1)
                for k in range(TPC):
                    j = g * TPC + k
                    last = nc.tensor.transpose(ps[:, 4 + g % 2, k * P:(k + 1) * P], T2[:, h, j * P:(j + 1) * P],
                                               ident[:, :])
                last.then_inc(pt2_ps, 1)

            def values2(r, h, g, first):
                if g == 0 and not first:
                    pe.wait_ge(att_rdy, r - 1)
                if g < NC - 1:
                    pe.wait_ge(pt2_act, r * 3 + g + 1)
                else:
                    pe.wait_ge(pt2_dve, r + 1)
                for k in range(TPC):
                    last = mm(ps[HD * k:HD * (k + 1), 6 + h % 2, 0:P], V[:, g * TPC + k, h * HD:(h + 1) * HD],
                              PT2[:, g, k * P:(k + 1) * P], start=(g == 0), stop=(g == NC - 1),
                              tile_position=(0, HD * k))
                if g == NC - 1:
                    last.then_inc(o2_ps, 1)

            def combine2(r, h):
                pe.wait_ge(o4_rdy, r + 1)
                mm(ps[:, 6 + h % 2, P:P + HD], o4[:, h % 2, :], sel[:, :], start=True, stop=True).then_inc(c2_ps, 1)

            def step2(b, s, t, h, u, loc=None):
                def there(lag):
                    return loc is None or 0 <= loc - lag < STEPS

                h2, h3 = ((h - k) % HEADS for k in (2, 3))
                if there(0):
                    scores2(b, s, t, h, u, loc == 0, loc is not None and loc < HEADS)
                if there(4):
                    combine2(s - 4, h)
                if there(3):
                    values2(s - 3, h3, 0, loc is not None and loc < 5)
                    values2(s - 3, h3, 1, False)
                if there(2):
                    if there(3):
                        pe.wait_ge(pt2_act, (s - 2) * 3)
                        pe.wait_ge(pt2_dve, s - 2)
                    probs_t2(s - 2, h2, 0)
                    probs_t2(s - 2, h2, 1)
                if there(3):
                    values2(s - 3, h3, 2, False)
                    values2(s - 3, h3, 3, False)
                if there(2):
                    pe.wait_ge(pt2_act, (s - 2) * 3 + 1)
                    probs_t2(s - 2, h2, 2)
                    pe.wait_ge(pt2_act, (s - 2) * 3 + 2)
                    probs_t2(s - 2, h2, 3)

            with pe.Fori(0, NB) as b:
                h_section(b, 0, 0, lambda g: project(b, 0, g))
                for l in range(LAYERS):
                    pe.wait_ge(hw_sb, b * (LAYERS * NC) + (l + 1) * NC)
                    if l == 0:
                        pe.wait_ge(adj_in, (b + 1) * (16 * NT))
                    for c in range(NC):
                        for t in range(NT):
                            last = mm(ps[:, c, :], HW[:, t * P:(t + 1) * P], A[:, t, c * CH:(c + 1) * CH],
                                      start=(t == 0), stop=(t == NT - 1))
                        last.then_inc(agg_ps, 1)
                        if c:
                            z_transposes(b, l, c - 1)
                    if l < LAYERS - 1:
                        h_section(b, l + 1, l + 1, lambda g: project(b, l + 1, g), lambda: z_transposes(b, l, NC - 1))
                    else:
                        z_transposes(b, l, NC - 1)
                h_section(b, LAYERS, LAYERS + 1, lambda c: mm(
                    ps[:, 4 + c, :], w1t2[:, :], HT[:, c * CH:(c + 1) * CH], start=True, stop=True).then_inc(qk1_ps, 1))
                pairs = HT[:, :].rearrange("p (g two) -> p g two", two=2)
                for c in range(2):
                    for two in range(2):
                        last = mm(ps[DG * two:DG * (two + 1), c, :], w2t[:, :], pairs[:, c * CH:(c + 1) * CH, two],
                                  start=True, stop=True, tile_position=(0, DG * two))
                    last.then_inc(qk1_ps, 1)
                pe.wait_ge(qk1_sb, (b + 1) * 6)
                tile1(b, 0, 0, False, True)
                tile1(b, 1, 1, True, True)
                with pe.Fori(1, NT // 2) as tt:
                    tile1(b, tt * 2, 0, True, False)
                    tile1(b, tt * 2 + 1, 1, True, False)
                probs_t1(b * NT + NT - 1, 1)
                out1(b * NT + NT - 1, 1)
                h_section(b, LAYERS + 1, LAYERS + 2, lambda c: mm(
                    ps[:, 4 + c, :], wq[:, :], HT[:, c * CH:(c + 1) * CH], start=True, stop=True).then_inc(qk2_ps, 1))
                for c in range(NC):
                    mm(ps[:, c, :], wk[:, :], HT[:, c * CH:(c + 1) * CH], start=True, stop=True).then_inc(qk2_ps, 1)
                pe.wait_ge(qk2_act, b * 8 + 4)
                for t in range(NT):
                    last = mm(ps[:, 4 + t // TPC, (t % TPC) * P:(t % TPC + 1) * P], HT[:, t * P:(t + 1) * P], wv[:, :],
                              start=True, stop=True)
                    if t % TPC == TPC - 1:
                        last.then_inc(v_ps, 1)
                pe.wait_ge(v_sb, (b + 1) * NC)
                pe.wait_ge(qk2_act, (b + 1) * 8)
                S0 = b * (NT * HEADS)
                for t in range(2):
                    for h in range(HEADS):
                        step2(b, S0 + t * HEADS + h, t, h, t, t * HEADS + h)
                with pe.Fori(1, NT // 2) as tt:
                    for u in range(2):
                        for h in range(HEADS):
                            step2(b, S0 + tt * (2 * HEADS) + (HEADS * u + h), tt * 2 + u, h, u)
                for loc in range(STEPS, STEPS + 4):
                    step2(b, S0 + loc, NT, loc % HEADS, 0, loc)
                pe.wait_ge(att_rdy, (b + 1) * (NT * HEADS))
                transposes(lambda t: H[:, t, :], 0, at_ps)
                for t in range(NT):
                    if t % TPC == 0:
                        pe.wait_ge(at_sb, b * NC + t // TPC + 1)
                    last = mm(ps[:, 4 + t // TPC, (t % TPC) * P:(t % TPC + 1) * P], HT[:, t * P:(t + 1) * P], wo[:, :],
                              start=True, stop=True)
                    if t % TPC == TPC - 1:
                        last.then_inc(x3_ps, 1)
                with pe.Fori(0, NT // 2) as tt:
                    for u in range(2):
                        T = b * NT + tt * 2 + u
                        pe.wait_ge(diag_rdy, b * NT + tt * 2 + (u + 1))
                        for j in range(NT):
                            g = j // TPC
                            if u and j == 2 * TPC:
                                pe.wait_ge(at3_act, T * 2)
                            last = nc.tensor.transpose(ps[:, (4 * u + g) % 6, (j % TPC) * P:(j % TPC + 1) * P],
                                                       ring[:, u, j * P:(j + 1) * P], ident[:, :])
                            if j % TPC == TPC - 1:
                                last.then_inc(at3_ps, 1)
                    for u in range(2):
                        T = b * NT + tt * 2 + u
                        AT = (AGG, HT)[u]
                        pe.wait_ge(g_rdy, b + 1)
                        pe.wait_ge(at3_act, (T + 1) * 2)
                        pe.wait_ge(at3_dve, (T + 1) * 2)
                        pe.wait_ge(o3_rdy, T + (NT + 2))
                        for j in range(NT):
                            last = mm(ps[:, 6 + u, 0:P], H[:, j, :], AT[:, j * P:(j + 1) * P],
                                      start=(j == 0), stop=(j == NT - 1))
                            if j == 0:
                                last.then_inc(ring_free, 1)
                        last.then_inc(hb_ps, 1)
                    for u in range(2):
                        T = b * NT + tt * 2 + u
                        pe.wait_ge(hb_sb, T + (NT + 1))
                        mm(ps[:, 6 + u, P:2 * P], hbT[:, u, :], wb[:, :], start=True, stop=True).then_inc(o3_ps, 1)


_INS = ["x", "adj", "L0_gnn_Ws", "L0_gnn_bs", "L0_gnn_gammas", "L0_gnn_betas", "L1_gnn_W1", "L1_gnn_W2", "L1_gnn_a",
        "L2_gnn_Wq", "L2_gnn_bq", "L2_gnn_Wk", "L2_gnn_bk", "L2_gnn_Wv", "L2_gnn_bv", "L2_gnn_Wo", "L2_gnn_bo",
        "L3_gnn_B"]


def kernel(**inputs):
    import numpy as np
    import concourse.bacc as bacc
    from concourse.bass_utils import run_bass_kernel_spmd

    nc = bacc.Bacc("TRN2", target_bir_lowering=False, num_devices=1)
    arrays, args = {}, []
    for name in _INS:
        a = np.ascontiguousarray(inputs[name])
        arrays[f"in_{name}"] = a
        args.append(nc.dram_tensor(f"in_{name}", a.shape, mybir.dt.from_np(a.dtype), kind="ExternalInput").ap())
    args.append(nc.dram_tensor("out_x", (NB, N, D), F32, kind="ExternalOutput").ap())
    build(nc, *args)
    r = run_bass_kernel_spmd(nc, [arrays], core_ids=[0])
    return r.results[0]["out_x"]
```
